# Optimizing a Trainium2 kernel written in Bass

```python
import numpy as np
import jax
import jax.numpy as jnp

def _softmax(x, axis=-1):
    return jax.nn.softmax(x, axis=axis)

def _gelu(x):
    return jax.nn.gelu(x, approximate=True)

def _silu(x):
    return jax.nn.silu(x)

def _sigmoid(x):
    return jax.nn.sigmoid(x)

def _layernorm(x, axis=-1, eps=1e-05):
    m = jnp.mean(x, axis=axis, keepdims=True)
    v = jnp.var(x, axis=axis, keepdims=True)
    return (x - m) / jnp.sqrt(v + eps)

def _scatter_add(tgt, idx, src, axis=0):
    return tgt.at[idx].add(src)

def _segment_sum(src, seg, n):
    return jax.ops.segment_sum(src, seg, n)
kernel_name = 'mk_xattn_seq_d4_seqx_r4_0c78a6'

def setup_inputs(seed: int=0):
    np.random.seed(seed)
    _w = jnp.asarray

    def _rec_inputs():
        import jax
        import jax.numpy as jnp
        _rk = jax.random.key(seed)
        x = 7.22e-05 + 1 * jax.random.normal(jax.random.fold_in(_rk, 1), (8, 256, 512), jnp.float32)
        _lenS = 256 - jax.random.randint(jax.random.fold_in(_rk, 7), (8,), 0, max(1, 256 // 4) + 1, jnp.int32)
        _lenS2 = 256 - jax.random.randint(jax.random.fold_in(_rk, 8), (8,), 0, max(1, 256 // 4) + 1, jnp.int32)
        _ctx_2048P = jax.random.normal(jax.random.fold_in(_rk, 11), (8, 16, 512), jnp.float32)
        _ctx_2048c = jax.random.dirichlet(jax.random.fold_in(_rk, 511), 0.3 * jnp.ones((16,), jnp.float32), (8, 256))
        _ctx_2048t = jnp.einsum('bsk,bkd->bsd', _ctx_2048c, _ctx_2048P)
        _ctx_2048t = _ctx_2048t * jax.lax.rsqrt(jnp.mean(jnp.square(_ctx_2048t)) + 1e-12) * 0.953939
        ctx_2048 = 2.81802e-05 + 1.00001 * (_ctx_2048t + 0.3 * jax.random.normal(jax.random.fold_in(_rk, 611), (8, 256, 512), jnp.float32))
        _validS = jnp.arange(256)[None, :] < _lenS[:, None]
        _validS2 = jnp.arange(256)[None, :] < _lenS2[:, None]
        _causal = jnp.tril(jnp.ones((256, 256), dtype=bool))
        mask_BxS2_bf1 = jnp.ones((8, 256), dtype=bool)
        mask_Bx1xSxS2_ff0 = jnp.where(jnp.ones((8, 1, 256, 256), dtype=bool), 0.0, -1000000000.0).astype(jnp.float32)
        return (x, ctx_2048, mask_BxS2_bf1, mask_Bx1xSxS2_ff0)
    x, ctx_2048, mask_BxS2_bf1, mask_Bx1xSxS2_ff0 = _rec_inputs()

    def _L0_xattn_setup():
        import jax, jax.numpy as jnp
        import numpy as np
        D = 512
        H = 16
        HD = D // H
        INNER = 4 * D
        EPS = 1e-05

        def layer_norm(x, w, b):
            mu = jnp.mean(x, axis=-1, keepdims=True)
            var = jnp.mean(jnp.square(x - mu), axis=-1, keepdims=True)
            return (x - mu) * jax.lax.rsqrt(var + EPS) * w + b
        key = jax.random.key(seed)
        ks = jax.random.split(key, 12)
        B, LQ, LK = (4, 256, 512)
        std = 0.02
        inp = {'hidden_states': jax.random.normal(ks[0], (B, LQ, D), jnp.float32), 'encoder_hidden_states': jax.random.normal(ks[1], (B, LK, D), jnp.float32), 'encoder_attention_mask': jnp.ones((B, LK), dtype=bool), 'ln1_w': jnp.ones((D,), jnp.float32), 'ln1_b': jnp.zeros((D,), jnp.float32), 'q_w': jax.random.normal(ks[2], (D, D), jnp.float32) * std, 'q_b': jnp.zeros((D,), jnp.float32), 'k_w': jax.random.normal(ks[3], (D, D), jnp.float32) * std, 'k_b': jnp.zeros((D,), jnp.float32), 'v_w': jax.random.normal(ks[4], (D, D), jnp.float32) * std, 'v_b': jnp.zeros((D,), jnp.float32), 'cproj_w': jax.random.normal(ks[5], (D, D), jnp.float32) * std, 'cproj_b': jnp.zeros((D,), jnp.float32), 'ln2_w': jnp.ones((D,), jnp.float32), 'ln2_b': jnp.zeros((D,), jnp.float32), 'fc_w': jax.random.normal(ks[6], (D, INNER), jnp.float32) * std, 'fc_b': jnp.zeros((INNER,), jnp.float32), 'proj_w': jax.random.normal(ks[7], (INNER, D), jnp.float32) * std, 'proj_b': jnp.zeros((D,), jnp.float32)}
        return inp
    _L0_xattn_all = _L0_xattn_setup()
    _L0_xattn_in = {k: v for k, v in _L0_xattn_all.items() if k in ('ln1_w', 'ln1_b', 'q_w', 'q_b', 'k_w', 'k_b', 'v_w', 'v_b', 'cproj_w', 'cproj_b', 'ln2_w', 'ln2_b', 'fc_w', 'fc_b', 'proj_w', 'proj_b')}
    del _L0_xattn_all

    def _L1_xattn_setup():
        import jax, jax.numpy as jnp
        import numpy as np
        H = 512
        B, L, S = (4, 1024, 10)
        key = jax.random.key(seed)
        k1, k2, k3, k4, k5, k6 = jax.random.split(key, 6)
        scale = 1.0 / np.sqrt(H)
        return {'h_english': jax.random.normal(k1, (B, L, H), dtype=jnp.float32), 'h_lojban': jax.random.normal(k2, (B, S, H), dtype=jnp.float32), 'w_q': jax.random.normal(k3, (H, H), dtype=jnp.float32) * scale, 'w_k': jax.random.normal(k4, (H, H), dtype=jnp.float32) * scale, 'w_v': jax.random.normal(k5, (H, H), dtype=jnp.float32) * scale, 'w_o': jax.random.normal(k6, (H, H), dtype=jnp.float32) * scale, 'alpha': jnp.float32(0.1)}
    _L1_xattn_all = _L1_xattn_setup()
    _L1_xattn_in = {k: v for k, v in _L1_xattn_all.items() if k in ('w_q', 'w_k', 'w_v', 'w_o', 'alpha')}
    del _L1_xattn_all

    def _L2_xattn_setup():
        import jax, jax.numpy as jnp
        import numpy as np
        H = 512
        NH = 32
        KVH = 8
        HD = H // NH
        GROUPS = NH // KVH
        EPS = 1e-06
        B, L, S = (4, 256, 256)

        def _gqa_forward(hidden_state, encoder_hidden_state, encoder_attention_mask, Wq, bq, Wk, bk, Wv, bv, Wo, bo, gamma, beta):
            b, l, _ = hidden_state.shape
            s = encoder_hidden_state.shape[1]
            q = hidden_state @ Wq + bq
            k = encoder_hidden_state @ Wk + bk
            v = encoder_hidden_state @ Wv + bv
            q = q.reshape(b, l, KVH, GROUPS, HD).transpose(0, 2, 3, 1, 4)
            k = k.reshape(b, s, KVH, HD).transpose(0, 2, 1, 3)
            v = v.reshape(b, s, KVH, HD).transpose(0, 2, 1, 3)
            scale = 1.0 / jnp.sqrt(jnp.asarray(HD, q.dtype))
            scores = jnp.einsum('bkgld,bksd->bkgls', q, k) * scale
            scores = scores + encoder_attention_mask[:, :, None, :, :]
            attn = jax.nn.softmax(scores, axis=-1)
            out = jnp.einsum('bkgls,bksd->bkgld', attn, v)
            out = out.transpose(0, 3, 1, 2, 4).reshape(b, l, H)
            out = out @ Wo + bo
            x = out + hidden_state
            mu = jnp.mean(x, axis=-1, keepdims=True)
            var = jnp.var(x, axis=-1, keepdims=True)
            return (x - mu) * jax.lax.rsqrt(var + EPS) * gamma + beta
        key = jax.random.key(seed)
        ks = jax.random.split(key, 12)
        sd = 0.02
        return {'hidden_state': jax.random.normal(ks[0], (B, L, H), jnp.float32), 'encoder_hidden_state': jax.random.normal(ks[1], (B, S, H), jnp.float32), 'encoder_attention_mask': jnp.zeros((B, 1, L, S), jnp.float32), 'Wq': jax.random.normal(ks[2], (H, H), jnp.float32) * sd, 'bq': jnp.zeros((H,), jnp.float32), 'Wk': jax.random.normal(ks[3], (H, KVH * HD), jnp.float32) * sd, 'bk': jnp.zeros((KVH * HD,), jnp.float32), 'Wv': jax.random.normal(ks[4], (H, KVH * HD), jnp.float32) * sd, 'bv': jnp.zeros((KVH * HD,), jnp.float32), 'Wo': jax.random.normal(ks[5], (H, H), jnp.float32) * sd, 'bo': jnp.zeros((H,), jnp.float32), 'gamma': jnp.ones((H,), jnp.float32), 'beta': jnp.zeros((H,), jnp.float32)}
    _L2_xattn_all = _L2_xattn_setup()
    _L2_xattn_in = {k: v for k, v in _L2_xattn_all.items() if k in ('Wq', 'bq', 'Wk', 'bk', 'Wv', 'bv', 'Wo', 'bo', 'gamma', 'beta')}
    del _L2_xattn_all

    def _L3_xattn_setup():
        import jax, jax.numpy as jnp
        import numpy as np
        HIDDEN = 512
        HEADS = 16
        HEAD_DIM = HIDDEN // HEADS
        LN_EPS = 1e-05
        GATE_INIT = 0.5

        def _layer_norm(x, gamma, beta):
            mu = jnp.mean(x, axis=-1, keepdims=True)
            var = jnp.mean(jnp.square(x - mu), axis=-1, keepdims=True)
            return (x - mu) * jax.lax.rsqrt(var + LN_EPS) * gamma + beta
        key = jax.random.key(seed)
        ks = jax.random.split(key, 8)
        B, T_TEXT, T_AUDIO = (4, 512, 375)
        s = 0.02
        return {'hidden_states': jax.random.normal(ks[0], (B, T_TEXT, HIDDEN), jnp.float32), 'audio_kv': jax.random.normal(ks[1], (B, T_AUDIO, HIDDEN), jnp.float32), 'audio_attention_mask': jnp.ones((B, T_AUDIO), dtype=bool), 'Wq': jax.random.normal(ks[2], (HIDDEN, HIDDEN), jnp.float32) * s, 'Wk': jax.random.normal(ks[3], (HIDDEN, HIDDEN), jnp.float32) * s, 'Wv': jax.random.normal(ks[4], (HIDDEN, HIDDEN), jnp.float32) * s, 'Wo': jax.random.normal(ks[5], (HIDDEN, HIDDEN), jnp.float32) * s, 'ln_gamma': jnp.ones((HIDDEN,), jnp.float32), 'ln_beta': jnp.zeros((HIDDEN,), jnp.float32), 'gate': jnp.array([GATE_INIT], jnp.float32)}
    _L3_xattn_all = _L3_xattn_setup()
    _L3_xattn_in = {k: v for k, v in _L3_xattn_all.items() if k in ('Wq', 'Wk', 'Wv', 'Wo', 'ln_gamma', 'ln_beta', 'gate')}
    del _L3_xattn_all
    return {'x': x, 'ctx_2048': ctx_2048, 'mask_BxS2_bf1': mask_BxS2_bf1, 'mask_Bx1xSxS2_ff0': mask_Bx1xSxS2_ff0, 'L0_xattn_ln1_w': _L0_xattn_in['ln1_w'], 'L0_xattn_ln1_b': _L0_xattn_in['ln1_b'], 'L0_xattn_q_w': _L0_xattn_in['q_w'], 'L0_xattn_q_b': _L0_xattn_in['q_b'], 'L0_xattn_k_w': _L0_xattn_in['k_w'], 'L0_xattn_k_b': _L0_xattn_in['k_b'], 'L0_xattn_v_w': _L0_xattn_in['v_w'], 'L0_xattn_v_b': _L0_xattn_in['v_b'], 'L0_xattn_cproj_w': _L0_xattn_in['cproj_w'], 'L0_xattn_cproj_b': _L0_xattn_in['cproj_b'], 'L0_xattn_ln2_w': _L0_xattn_in['ln2_w'], 'L0_xattn_ln2_b': _L0_xattn_in['ln2_b'], 'L0_xattn_fc_w': _L0_xattn_in['fc_w'], 'L0_xattn_fc_b': _L0_xattn_in['fc_b'], 'L0_xattn_proj_w': _L0_xattn_in['proj_w'], 'L0_xattn_proj_b': _L0_xattn_in['proj_b'], 'L1_xattn_w_q': _L1_xattn_in['w_q'], 'L1_xattn_w_k': _L1_xattn_in['w_k'], 'L1_xattn_w_v': _L1_xattn_in['w_v'], 'L1_xattn_w_o': _L1_xattn_in['w_o'], 'L1_xattn_alpha': _L1_xattn_in['alpha'], 'L2_xattn_Wq': _L2_xattn_in['Wq'], 'L2_xattn_bq': _L2_xattn_in['bq'], 'L2_xattn_Wk': _L2_xattn_in['Wk'], 'L2_xattn_bk': _L2_xattn_in['bk'], 'L2_xattn_Wv': _L2_xattn_in['Wv'], 'L2_xattn_bv': _L2_xattn_in['bv'], 'L2_xattn_Wo': _L2_xattn_in['Wo'], 'L2_xattn_bo': _L2_xattn_in['bo'], 'L2_xattn_gamma': _L2_xattn_in['gamma'], 'L2_xattn_beta': _L2_xattn_in['beta'], 'L3_xattn_Wq': _L3_xattn_in['Wq'], 'L3_xattn_Wk': _L3_xattn_in['Wk'], 'L3_xattn_Wv': _L3_xattn_in['Wv'], 'L3_xattn_Wo': _L3_xattn_in['Wo'], 'L3_xattn_ln_gamma': _L3_xattn_in['ln_gamma'], 'L3_xattn_ln_beta': _L3_xattn_in['ln_beta'], 'L3_xattn_gate': _L3_xattn_in['gate']}

def reference(x, ctx_2048, mask_BxS2_bf1, mask_Bx1xSxS2_ff0, L0_xattn_ln1_w, L0_xattn_ln1_b, L0_xattn_q_w, L0_xattn_q_b, L0_xattn_k_w, L0_xattn_k_b, L0_xattn_v_w, L0_xattn_v_b, L0_xattn_cproj_w, L0_xattn_cproj_b, L0_xattn_ln2_w, L0_xattn_ln2_b, L0_xattn_fc_w, L0_xattn_fc_b, L0_xattn_proj_w, L0_xattn_proj_b, L1_xattn_w_q, L1_xattn_w_k, L1_xattn_w_v, L1_xattn_w_o, L1_xattn_alpha, L2_xattn_Wq, L2_xattn_bq, L2_xattn_Wk, L2_xattn_bk, L2_xattn_Wv, L2_xattn_bv, L2_xattn_Wo, L2_xattn_bo, L2_xattn_gamma, L2_xattn_beta, L3_xattn_Wq, L3_xattn_Wk, L3_xattn_Wv, L3_xattn_Wo, L3_xattn_ln_gamma, L3_xattn_ln_beta, L3_xattn_gate):
    import jax
    import jax.numpy as jnp

    def _L0_xattn_ref(hidden_states, encoder_hidden_states, encoder_attention_mask, ln1_w, ln1_b, q_w, q_b, k_w, k_b, v_w, v_b, cproj_w, cproj_b, ln2_w, ln2_b, fc_w, fc_b, proj_w, proj_b):
        import jax, jax.numpy as jnp
        import numpy as np
        D = 512
        H = 16
        HD = D // H
        INNER = 4 * D
        EPS = 1e-05

        def layer_norm(x, w, b):
            mu = jnp.mean(x, axis=-1, keepdims=True)
            var = jnp.mean(jnp.square(x - mu), axis=-1, keepdims=True)
            return (x - mu) * jax.lax.rsqrt(var + EPS) * w + b
        B, LQ, _ = hidden_states.shape
        LK = encoder_hidden_states.shape[1]
        residual = hidden_states
        x = layer_norm(hidden_states, ln1_w, ln1_b)
        q = (x @ q_w + q_b).reshape(B, LQ, H, HD).transpose(0, 2, 1, 3)
        k = (encoder_hidden_states @ k_w + k_b).reshape(B, LK, H, HD).transpose(0, 2, 1, 3)
        v = (encoder_hidden_states @ v_w + v_b).reshape(B, LK, H, HD).transpose(0, 2, 1, 3)
        scale = 1.0 / np.sqrt(HD).astype(np.float32)
        scores = jnp.einsum('bhqd,bhkd->bhqk', q, k) * scale
        mask = encoder_attention_mask[:, None, None, :]
        mask_value = jnp.finfo(scores.dtype).min
        scores = jnp.where(mask, scores, mask_value)
        attn = jax.nn.softmax(scores, axis=-1)
        out = jnp.einsum('bhqk,bhkd->bhqd', attn, v)
        out = out.transpose(0, 2, 1, 3).reshape(B, LQ, D)
        out = out @ cproj_w + cproj_b
        hidden = out + residual
        residual = hidden
        y = layer_norm(hidden, ln2_w, ln2_b)
        y = jax.nn.gelu(y @ fc_w + fc_b, approximate=True)
        y = y @ proj_w + proj_b
        return residual + y

    def _L1_xattn_ref(h_english, h_lojban, w_q, w_k, w_v, w_o, alpha):
        import jax, jax.numpy as jnp
        import numpy as np
        H = 512
        B, L, S = (4, 1024, 10)
        h = h_english.shape[-1]
        q = jnp.einsum('blh,oh->blo', h_english, w_q)
        k = jnp.einsum('bsh,oh->bso', h_lojban, w_k)
        v = jnp.einsum('bsh,oh->bso', h_lojban, w_v)
        scores = jnp.einsum('blh,bsh->bls', q, k) / jnp.sqrt(jnp.float32(h))
        probs = jax.nn.softmax(scores, axis=-1)
        context = jnp.einsum('bls,bsh->blh', probs, v)
        delta = jnp.einsum('blh,oh->blo', context, w_o)
        return h_english + alpha * delta

    def _L2_xattn_ref(hidden_state, encoder_hidden_state, encoder_attention_mask, Wq, bq, Wk, bk, Wv, bv, Wo, bo, gamma, beta):
        import jax, jax.numpy as jnp
        import numpy as np
        H = 512
        NH = 32
        KVH = 8
        HD = H // NH
        GROUPS = NH // KVH
        EPS = 1e-06
        B, L, S = (4, 256, 256)

        def _gqa_forward(hidden_state, encoder_hidden_state, encoder_attention_mask, Wq, bq, Wk, bk, Wv, bv, Wo, bo, gamma, beta):
            b, l, _ = hidden_state.shape
            s = encoder_hidden_state.shape[1]
            q = hidden_state @ Wq + bq
            k = encoder_hidden_state @ Wk + bk
            v = encoder_hidden_state @ Wv + bv
            q = q.reshape(b, l, KVH, GROUPS, HD).transpose(0, 2, 3, 1, 4)
            k = k.reshape(b, s, KVH, HD).transpose(0, 2, 1, 3)
            v = v.reshape(b, s, KVH, HD).transpose(0, 2, 1, 3)
            scale = 1.0 / jnp.sqrt(jnp.asarray(HD, q.dtype))
            scores = jnp.einsum('bkgld,bksd->bkgls', q, k) * scale
            scores = scores + encoder_attention_mask[:, :, None, :, :]
            attn = jax.nn.softmax(scores, axis=-1)
            out = jnp.einsum('bkgls,bksd->bkgld', attn, v)
            out = out.transpose(0, 3, 1, 2, 4).reshape(b, l, H)
            out = out @ Wo + bo
            x = out + hidden_state
            mu = jnp.mean(x, axis=-1, keepdims=True)
            var = jnp.var(x, axis=-1, keepdims=True)
            return (x - mu) * jax.lax.rsqrt(var + EPS) * gamma + beta
        return _gqa_forward(hidden_state, encoder_hidden_state, encoder_attention_mask, Wq, bq, Wk, bk, Wv, bv, Wo, bo, gamma, beta)

    def _L3_xattn_ref(hidden_states, audio_kv, audio_attention_mask, Wq, Wk, Wv, Wo, ln_gamma, ln_beta, gate):
        import jax, jax.numpy as jnp
        import numpy as np
        HIDDEN = 512
        HEADS = 16
        HEAD_DIM = HIDDEN // HEADS
        LN_EPS = 1e-05
        GATE_INIT = 0.5

        def _layer_norm(x, gamma, beta):
            mu = jnp.mean(x, axis=-1, keepdims=True)
            var = jnp.mean(jnp.square(x - mu), axis=-1, keepdims=True)
            return (x - mu) * jax.lax.rsqrt(var + LN_EPS) * gamma + beta
        B, Tt, D = hidden_states.shape
        Ta = audio_kv.shape[1]
        scale = HEAD_DIM ** (-0.5)
        a = _layer_norm(audio_kv, ln_gamma, ln_beta)
        Q = (hidden_states @ Wq.T).reshape(B, Tt, HEADS, HEAD_DIM).transpose(0, 2, 1, 3)
        K = (a @ Wk.T).reshape(B, Ta, HEADS, HEAD_DIM).transpose(0, 2, 1, 3)
        V = (a @ Wv.T).reshape(B, Ta, HEADS, HEAD_DIM).transpose(0, 2, 1, 3)
        scores = jnp.einsum('bhtd,bhsd->bhts', Q, K) * scale
        mask = audio_attention_mask[:, None, None, :]
        scores = jnp.where(mask, scores, jnp.float32(-jnp.inf))
        attn = jax.nn.softmax(scores, axis=-1)
        out = jnp.einsum('bhts,bhsd->bhtd', attn, V)
        out = out.transpose(0, 2, 1, 3).reshape(B, Tt, D)
        out = out @ Wo.T
        return hidden_states + jnp.tanh(gate) * out
    x = _L0_xattn_ref(x, ctx_2048, mask_BxS2_bf1, L0_xattn_ln1_w, L0_xattn_ln1_b, L0_xattn_q_w, L0_xattn_q_b, L0_xattn_k_w, L0_xattn_k_b, L0_xattn_v_w, L0_xattn_v_b, L0_xattn_cproj_w, L0_xattn_cproj_b, L0_xattn_ln2_w, L0_xattn_ln2_b, L0_xattn_fc_w, L0_xattn_fc_b, L0_xattn_proj_w, L0_xattn_proj_b)
    x = _L1_xattn_ref(x, ctx_2048, L1_xattn_w_q, L1_xattn_w_k, L1_xattn_w_v, L1_xattn_w_o, L1_xattn_alpha)
    x = _L2_xattn_ref(x, ctx_2048, mask_Bx1xSxS2_ff0, L2_xattn_Wq, L2_xattn_bq, L2_xattn_Wk, L2_xattn_bk, L2_xattn_Wv, L2_xattn_bv, L2_xattn_Wo, L2_xattn_bo, L2_xattn_gamma, L2_xattn_beta)
    x = _L3_xattn_ref(x, ctx_2048, mask_BxS2_bf1, L3_xattn_Wq, L3_xattn_Wk, L3_xattn_Wv, L3_xattn_Wo, L3_xattn_ln_gamma, L3_xattn_ln_beta, L3_xattn_gate)
    return x

_drawn_inputs = setup_inputs


def setup_inputs(seed=0):
    import zlib

    import numpy as np

    out = dict(_drawn_inputs(seed))
    spreads = {'L0_xattn_ln1_w': (1.0, 0.6),
     'L0_xattn_ln1_b': (0.0, 0.8),
     'L0_xattn_q_b': (0.0, 0.8),
     'L0_xattn_k_b': (0.0, 0.8),
     'L0_xattn_v_b': (0.0, 0.1),
     'L0_xattn_cproj_b': (0.0, 0.1),
     'L0_xattn_ln2_w': (1.0, 0.2),
     'L0_xattn_ln2_b': (0.0, 0.345),
     'L0_xattn_fc_b': (0.0, 0.1),
     'L0_xattn_proj_b': (0.0, 0.1),
     'L2_xattn_bq': (0.0, 0.8),
     'L2_xattn_bk': (0.0, 0.8),
     'L2_xattn_bv': (0.0, 0.1),
     'L2_xattn_bo': (0.0, 0.1),
     'L2_xattn_gamma': (1.0, 0.2),
     'L2_xattn_beta': (0.0, 0.1),
     'L3_xattn_ln_gamma': (1.0, 0.6),
     'L3_xattn_ln_beta': (0.0, 0.8)}
    factors = {'L0_xattn_q_w': 7.398,
     'L0_xattn_k_w': 7.244,
     'L1_xattn_w_q': 2.869,
     'L1_xattn_w_k': 2.939,
     'L2_xattn_Wq': 7.546,
     'L2_xattn_Wk': 7.406,
     'L3_xattn_Wq': 8.0,
     'L3_xattn_Wk': 8.0}
    for name, (base, spread) in spreads.items():
        noise = np.random.default_rng([zlib.crc32(name.encode()), seed]).standard_normal(out[name].shape)
        drawn = base * np.exp(spread * noise) if base else spread * noise
        out[name] = jnp.asarray(drawn.astype(out[name].dtype))
    for name, factor in factors.items():
        out[name] = (out[name] * factor).astype(out[name].dtype)
    return out
```

```python
from contextlib import ExitStack

import concourse.bass as bass
from concourse import mybir

F32 = mybir.dt.float32
F32R = mybir.dt.float32r
U8 = mybir.dt.uint8
ALU = mybir.AluOpType
ACT = mybir.ActivationFunctionType
AX_X = mybir.AxisListType.X

P = 128
D = 512
KC = D // P
NB = 8
S = 256
TT = S // P
INNER = 4 * D
BANK = 512
STEPS = 4
HI, LO = 0, 1
MASKED = -(2.0 ** 127)
PAIRS = ((HI, HI), (HI, LO), (LO, HI))


def wait(eng, sem, value):
    if isinstance(value, int) and value <= 0:
        return
    eng.wait_ge(sem, value)


def rows_of(x, b):
    return x[bass.ds(b * S, S)].rearrange("(t p) n -> p t n", p=P)


class Buffers:

    def __init__(self, nc, ctx, tag):
        self.nc, self.ctx, self.tag, self.sems = nc, ctx, tag, []
        ctx.callback(self.clear)

    def sb(self, name, shape, dt=F32):
        return self.ctx.enter_context(self.nc.sbuf_tensor(f"{self.tag}_{name}", shape, dt))

    def sem(self, name):
        self.sems.append(self.nc.alloc_semaphore(name=f"{self.tag}_{name}"))
        return self.sems[-1]

    def clear(self):
        self.nc.clear_and_free_semaphores(self.sems)
        self.nc.all_engine_barrier()


def setup_phase(nc, c, A):
    with ExitStack() as ctx:
        al = Buffers(nc, ctx, "set")
        stage = al.sb("vec_rows", [32, P])
        m8 = al.sb("m8", [NB, S], U8)
        m0 = al.sb("m0", [NB, S])
        m1 = al.sb("m1", [NB, S])
        any_key, guard = al.sb("any_key", [NB, 1]), al.sb("guard", [NB, 1])
        any_done = al.sem("any_done")
        loaded, zeroed, ident_done = al.sem("loaded"), al.sem("zeroed"), al.sem("ident_done")
        turned, cols_done, m0_done, m1_done, stored = (al.sem(n) for n in ("turned", "cols_done", "m0_done", "m1_done", "stored"))
        block = ctx.enter_context(nc.Block())
        vecs = [("L0_xattn_q_b", 4), ("L0_xattn_k_b", 4), ("L2_xattn_bq", 4), ("L2_xattn_bk", 1), ("L0_xattn_fc_b", 16)]

        @block.sync
        def _(sp):
            row = 0
            for name, n in vecs:
                sp.dma_start(stage[row:row + n, :], A[name].rearrange("(r p) -> r p", p=P)).then_inc(loaded, 16)
                c["col"][name] = row
                row += n
            sp.dma_start(m8[:], A["mask_BxS2_bf1"]).then_inc(loaded, 16)
            sp.wait_ge(m0_done, 1)
            for h in range(4):
                sp.dma_start(c["mask_min"][:, h * S:(h + 1) * S], m0[:]).then_inc(stored, 16)
            sp.wait_ge(m1_done, 1)
            for h in range(4):
                sp.dma_start(c["mask_inf"][:, h * S:(h + 1) * S], m1[:]).then_inc(stored, 16)
            sp.wait_ge(stored, 8 * 16)

        @block.gpsimd
        def _(pool):
            nc.gpsimd.memset(c["half"][:], -0.5)
            nc.gpsimd.memset(c["ident"][:], 0.0).then_inc(zeroed, 1)
            pool.wait_ge(zeroed, 1)
            nc.gpsimd.affine_select(out=c["ident"][:], in_=c["ident"][:], compare_op=ALU.not_equal, fill=1.0,
                                    base=0, pattern=[[-1, P]], channel_multiplier=1).then_inc(ident_done, 1)

        @block.tensor
        def _(pe):
            pe.wait_ge(loaded, 16 * (len(vecs) + 1))
            pe.wait_ge(ident_done, 1)
            nc.tensor.transpose(c["ps"][:, 0, 0:29], stage[0:29, :], c["ident"][0:29, 0:29]).then_inc(turned, 1)

        @block.vector
        def _(dve):
            dve.wait_ge(turned, 1)
            nc.vector.tensor_copy(c["cols"][:, 0:29], c["ps"][:, 0, 0:29]).then_inc(cols_done, 1)
            dve.wait_ge(cols_done, 1)
            nc.vector.tensor_scalar(c["cols"][:, 0:4], c["cols"][:, 0:4], 32.0 ** -0.5, None, ALU.mult)
            nc.vector.tensor_scalar(c["cols"][:, 8:12], c["cols"][:, 8:12], 0.25, None, ALU.mult)
            dve.wait_ge(loaded, 16 * (len(vecs) + 1))
            nc.vector.tensor_scalar(m0[:], m8[:], -1.0, -MASKED, ALU.add, ALU.mult).then_inc(m0_done, 1)
            dve.wait_ge(m0_done, 1)
            nc.vector.tensor_reduce(any_key[:], m8[:], AX_X, ALU.max).then_inc(any_done, 1)
            dve.wait_ge(any_done, 1)
            nc.vector.reciprocal(guard[:], any_key[:]).then_inc(any_done, 1)
            dve.wait_ge(any_done, 2)
            nc.vector.scalar_tensor_tensor(guard[:], any_key[:], guard[:, 0:1], any_key[:], ALU.mult, ALU.subtract).then_inc(any_done, 1)
            dve.wait_ge(any_done, 3)
            nc.vector.tensor_scalar(m1[:], m0[:], guard[:, 0:1], None, ALU.add).then_inc(m1_done, 1)


def attention_phase(nc, c, A, L):
    x_in, x_out, ctx_in = L["x_in"], L["x_out"], A["ctx_2048"]
    HS, HD, GQA = L["heads"] // STEPS, L["hd"], L["gqa"]
    NPAIR = HS // 2
    NK = L["nk"]
    BASE = 3 * HD
    KROWS = BASE if GQA else BASE + 1
    UNITS = 2 * NPAIR
    W_T = L["transposed"]
    post_ln, ln_x, ln_c = L["post_ln"], L["ln_x"], L["ln_c"]
    has_ln = ln_x or ln_c
    ps, ident = c["ps"], c["ident"]
    B_QK, B_OT, B_A, B_PT = 0, 3, 4, 6
    T_BANK = {("y", 0): 2, ("y", 1): 1, ("BT", 0): 2, ("O", 0): 1, ("BT", 1): 2, ("O", 1): 1, ("BT", 2): 2,
              ("V", 0): 1, ("x", 0): B_QK, ("x", 1): 2, ("V", 1): 1, ("BT", 3): B_QK, ("c", 0): 2, ("c", 1): 1}

    with ExitStack() as ctx:
        al = Buffers(nc, ctx, L["tag"])
        wq = al.sb("wq", [P, 2, KC, D], F32R)
        wk = al.sb("wk", [P, 2, KC, NK], F32R)
        wv = al.sb("wv", [P, 2, KC, NK], F32R)
        wo = al.sb("wo", [P, 2, KC, D], F32R)
        xin = al.sb("xin", [P, TT, D])
        cin = al.sb("cin", [P, TT, D])
        norm = al.sb("norm", [P, TT, D]) if has_ln else None
        xsrc = norm if ln_x else xin
        csrc = norm if ln_c else cin
        xT = al.sb("xT", [P, 2, KC, S], F32R)
        cT = al.sb("cT", [P, 2, KC, S], F32R)
        yT = al.sb("yT", [P, 2, KC, S], F32R)
        NE = 2 if GQA else 4
        E = al.sb("E", [P, 2, NE, S], F32R)
        EK = al.sb("EK", [P, 2, S], F32R) if GQA else None
        if GQA:
            qst = al.sb("qst", [64, STEPS, HS, S], F32R)
            kst = al.sb("kst", [64, STEPS, 2, S], F32R)
            V = al.sb("V", [P, TT, NK // HD, 32])
            mask_next, maskN = al.sb("mask_next", [P, TT, S]), al.sb("maskN", [P, TT, S])
        else:
            st = al.sb("st", [P, STEPS, HS, 2, S], F32R)
            V = al.sb("V", [P, TT, D])
        Pb = al.sb("Pb", [P, TT, HS, S])
        PTb = al.sb("PTb", [P, 2, TT, HS, S])
        OTs = al.sb("OTs", [P, BANK])
        y = al.sb("y", [P, TT, D])
        xres = al.sb("xres", [P, TT, D])
        xo = al.sb("xo", [P, TT, D])
        rows = {n: al.sb(f"row{i}", [P, w]) for i, (n, _, w) in enumerate(L["rows"])}
        negmax = al.sb("negmax", [P, TT, HS])
        nposmax = al.sb("nposmax", [P, TT, HS])
        sums = al.sb("sums", [P, STEPS, TT, HS])
        rcp2 = al.sb("rcp", [P, 2, 16])
        dummy = al.sb("dummy", [P, UNITS + 1])
        eps = al.sb("eps", [P, TT])
        stats = al.sb("stats", [P, TT, 6])
        mv = al.sb("mv", [P, TT, 2])
        veps = al.sb("veps", [P, TT])
        rstd = al.sb("rstd", [P, TT])
        pstats = al.sb("pstats", [P, TT, 6])
        pmv = al.sb("pmv", [P, TT, 2])
        pveps = al.sb("pveps", [P, TT])
        prstd = al.sb("prstd", [P, TT])
        gate = al.sb("gate", [P, 2])

        sem = {}
        for n in ("w_in0 w_in1 row_in gate_in gate_done wT_mm w_hi w_lo x_in c_in xres_in mask_in out_st ek_w "
                  "pe_T act_hi dve_T pe_qk act_e dve_e pe_a dve_max act_exp pe_pt act_pt dve_pt pe_pv act_ot "
                  "dve_bs dve_mv pool_ve pool_rs dve_xn pool_g pool_b pool_res dve_rc dve_pbs dve_pmv "
                  "eps_set pool_pve pool_prs dve_pxn pool_pg pool_out ones_done dve_mask").split():
            sem[n] = al.sem(n)
        e_written = [al.sem(f"e_written{i}") for i in range(2)]
        stacked = [al.sem(f"stacked{g}") for g in range(STEPS)]
        block = ctx.enter_context(nc.Block())

        LOOP = 2
        front, back, outp, nxt = (lambda v: v < NB), (lambda v: 1 <= v <= NB), (lambda v: v >= 2), (lambda v: v < NB - 1)

        def items(v):
            if v < 0:
                return [("x", 0), ("x", 1), ("c", 0), ("c", 1)]
            has = {"y": outp(v), "O": outp(v), "BT": back(v), "V": front(v), "x": nxt(v), "c": nxt(v)}
            out = [k for k in T_BANK if has[k[0]]]
            return out

        def count(v, of=len):
            return sum(of(items(w)) for w in range(-1, v))

        def turned(seq):
            return sum(k in "xyc" for k, _ in seq)

        def ahead(v, u, of=len):
            return u * of(items(LOOP)) + count(LOOP, of) if v == LOOP else count(v, of)

        def item_no(v, u, key):
            return ahead(v, u) + items(v).index(key)

        def turn_no(v, u, key):
            return ahead(v, u, turned) + turned(items(v)[:items(v).index(key)])

        def before_in_bank(v, u, key):
            seq = items(v)
            i = seq.index(key)
            same = [j for j in range(i) if T_BANK[seq[j]] == T_BANK[key]]
            if same:
                return ahead(v, u) + same[-1] + 1
            prev = items(v - 1)
            same = [j for j, k in enumerate(prev) if T_BANK[k] == T_BANK[key]]
            return ahead(v, u) - (len(prev) - 1 - same[-1]) if same else ahead(v, u)

        def bodies(eng, body):
            body(0, 0, None, None, 0)
            body(1, 1, 0, None, 0)
            with eng.Fori(0, NB - 1 - LOOP) as u:
                body(LOOP, u + 2, u + 1, u, u)
            body(NB - 1, NB - 1, NB - 2, NB - 3, 0)
            body(NB, None, NB - 1, NB - 2, 0)
            body(NB + 1, None, None, NB - 1, 0)

        def back_step(vf, vb, g, lag):
            b, gg = (vf, g - lag) if g >= lag else (vb, g - lag + STEPS)
            return None if b is None else (b, gg)

        def unit(b, g, i):
            return b * (STEPS * UNITS) + (g * UNITS + i)

        wunits = [("q", A[L["wq"]], wq, D, L["qscale"]), ("k", A[L["wk"]], wk, NK, 1.0),
                  ("v", A[L["wv"]], wv, NK, 1.0), ("o", A[L["wo"]], wo, D, L["oscale"])]
        stages = [Pb[:].rearrange("p a b c -> p (a b c)"), PTb[:].rearrange("p i a b c -> p (i a b c)")]

        def stage_of(j, n):
            return stages[j % 2][:, 0:KC * n].rearrange("p (k n) -> p k n", k=KC)

        n_reads = 6 if GQA else 5

        @block.sync
        def _(sp):
            sp.dma_start(xin[:], rows_of(x_in, 0)).then_inc(sem["x_in"], 16)
            sp.dma_start(cin[:], rows_of(ctx_in, 0)).then_inc(sem["c_in"], 16)
            for n, src, w in L["rows"]:
                sp.dma_start(rows[n][:], A[src].partition_broadcast(P)).then_inc(sem["row_in"], 16)
            if L["oscale"] is None:
                sp.dma_start(gate[:, 0:1], A["L3_xattn_gate"].partition_broadcast(P)).then_inc(sem["gate_in"], 16)
            for j, (_, src, _, n, _) in enumerate(wunits):
                if j >= 2:
                    sp.wait_ge(sem["w_lo"], j - 1)
                sp.dma_start(stage_of(j, n), src.rearrange("(k p) n -> p k n", p=P)).then_inc(sem[f"w_in{j % 2}"], 16)

            def body(v, vf, vb, vo, u):
                F, B, O, N = front(v), back(v), outp(v), nxt(v)
                if N:
                    sp.wait_ge(sem["pe_T"], ahead(v, u))
                    if has_ln:
                        wait(sp, sem["dve_xn"], vf * TT + TT)
                    sp.dma_start(xin[:], rows_of(x_in, vf + 1)).then_inc(sem["x_in"], 16)
                    sp.dma_start(cin[:], rows_of(ctx_in, vf + 1)).then_inc(sem["c_in"], 16)
                if O:
                    if post_ln:
                        wait(sp, sem["dve_pxn"], vo * TT)
                    else:
                        sp.wait_ge(sem["dve_T"], ahead(v, u))
                    sp.dma_start(xres[:], rows_of(x_in, vo)).then_inc(sem["xres_in"], 16)
                if GQA and F:
                    wait(sp, sem["dve_mask"], vf)
                    sp.dma_start(mask_next[:], A["mask_Bx1xSxS2_ff0"][bass.ds(vf * S, S)].rearrange(
                        "(t p) k -> p t k", p=P)).then_inc(sem["mask_in"], 16)
                for g in range(STEPS):
                    if not F:
                        continue
                    par = g % 2
                    sp.wait_ge(sem["act_e"], (vf * STEPS + g) + 1)
                    sp.wait_ge(sem["dve_e"], (vf * STEPS + g) + 1)
                    scr = c["scr"][g]
                    sp.dma_start(scr[:, 0:NE, :], E[:, par].bitcast(F32)).then_inc(e_written[par], 16)
                    if GQA and g == 0:
                        filled = vf * (16 * n_reads)
                        for gg in range(STEPS):
                            wait(sp, stacked[gg], filled)
                        sp.dma_start(c["scrk"], EK[:].bitcast(F32)).then_inc(sem["ek_w"], 16)
                        sp.wait_ge(sem["ek_w"], vf * 16 + 16)
                    written = (vf * 2 + g // 2) * 16 + 16
                    if B:
                        sp.wait_ge(sem["pe_a"], unit(vb, g, UNITS))
                    sp.wait_ge(e_written[par], written)
                    if GQA:
                        q = [scr[:, j, :].rearrange("(h d) t -> d h t", d=HD) for j in range(2)]
                        k = [c["scrk"][2 * HD * g:2 * HD * (g + 1), j, :].rearrange("(h d) t -> d h t", d=HD) for j in range(2)]
                        for r, (jq, jk) in enumerate(PAIRS):
                            pr = slice(r * HD, (r + 1) * HD)
                            sp.dma_start(qst[pr, g].bitcast(F32), q[jq]).then_inc(stacked[g], 16)
                            sp.dma_start(kst[pr, g].bitcast(F32), k[jk]).then_inc(stacked[g], 16)
                    else:
                        split = scr.rearrange("(h d) j t -> d h j t", d=HD)
                        sp.dma_start(st[0:HD, g, :, 0, :].bitcast(F32), split[:, :, 0, :]).then_inc(stacked[g], 16)
                        sp.dma_start(st[0:HD, g, :, 1, :].bitcast(F32), split[:, :, 3, :]).then_inc(stacked[g], 16)
                        sp.dma_start(st[HD:2 * HD, g].bitcast(F32), split[:, :, 0:2, :]).then_inc(stacked[g], 16)
                        sp.dma_start(st[2 * HD:3 * HD, g].bitcast(F32), split[:, :, 2:4, :]).then_inc(stacked[g], 16)
                        sp.dma_start(st[3 * HD:3 * HD + 1, g, :, 1, :].bitcast(F32),
                                     L["mask"][bass.ds(vf, 1)].rearrange("b (h t) -> b h t", h=HS)).then_inc(stacked[g], 16)
                if O:
                    if post_ln:
                        sp.wait_ge(sem["pool_out"], vo * TT + TT)
                    else:
                        sp.wait_ge(sem["dve_T"], item_no(v, u, ("O", 1)) + 1)
                    sp.dma_start(rows_of(x_out, vo), xo[:]).then_inc(sem["out_st"], 16)

            bodies(sp, body)
            sp.wait_ge(sem["out_st"], 16 * NB)

        @block.gpsimd
        def _(pool):
            nc.gpsimd.memset(eps[:], L["eps"]).then_inc(sem["eps_set"], 1)
            pool.wait_ge(sem["eps_set"], 1)
            if GQA:
                nc.gpsimd.memset(V[:], 1.0).then_inc(sem["ones_done"], 1)
            else:
                nc.gpsimd.memset(st[3 * HD:3 * HD + 1, :, :, 0, :].bitcast(F32), 1.0).then_inc(sem["ones_done"], 1)
            pool.wait_ge(sem["ones_done"], 1)
            pool.wait_ge(sem["row_in"], 16 * len(L["rows"]))

            def norm_rows(n):
                pool.wait_ge(sem["dve_mv"], n * TT + TT)
                nc.gpsimd.tensor_tensor(veps[:], mv[:, :, 1], eps[:], ALU.add).then_inc(sem["pool_ve"], 1)
                pool.wait_ge(sem["pool_ve"], n + 1)
                nc.gpsimd.tensor_tensor(rstd[:], veps[:], c["half"][:, 0:TT], ALU.pow).then_inc(sem["pool_rs"], 1)
                for t in range(TT):
                    pool.wait_ge(sem["dve_xn"], n * TT + (t + 1))
                    nc.gpsimd.tensor_tensor(norm[:, t], norm[:, t], rows["g"][:], ALU.mult).then_inc(sem["pool_g"], 1)
                    pool.wait_ge(sem["pool_g"], n * TT + (t + 1))
                    nc.gpsimd.tensor_tensor(norm[:, t], norm[:, t], rows["b"][:], ALU.add).then_inc(sem["pool_b"], 1)

            if has_ln:
                norm_rows(0)

            def body(v, vf, vb, vo, u):
                if outp(v):
                    pool.wait_ge(sem["xres_in"], vo * 16 + 16)
                    for t in range(TT):
                        if "ob" in rows:
                            nc.gpsimd.tensor_tensor(xres[:, t], xres[:, t], rows["ob"][:], ALU.add).then_inc(sem["pool_res"], 1)
                if has_ln and nxt(v):
                    norm_rows(vf + 1)
                if outp(v) and post_ln:
                    pool.wait_ge(sem["dve_pmv"], vo * TT + TT)
                    nc.gpsimd.tensor_tensor(pveps[:], pmv[:, :, 1], eps[:], ALU.add).then_inc(sem["pool_pve"], 1)
                    pool.wait_ge(sem["pool_pve"], vo + 1)
                    nc.gpsimd.tensor_tensor(prstd[:], pveps[:], c["half"][:, 0:TT], ALU.pow).then_inc(sem["pool_prs"], 1)
                    for t in range(TT):
                        pool.wait_ge(sem["dve_pxn"], vo * TT + (t + 1))
                        nc.gpsimd.tensor_tensor(xo[:, t], xo[:, t], rows["g"][:], ALU.mult).then_inc(sem["pool_pg"], 1)
                        pool.wait_ge(sem["pool_pg"], vo * TT + (t + 1))
                        nc.gpsimd.tensor_tensor(xo[:, t], xo[:, t], rows["b"][:], ALU.add).then_inc(sem["pool_out"], 1)

            bodies(pool, body)

        @block.scalar
        def _(act):
            if L["oscale"] is None:
                act.wait_ge(sem["gate_in"], 16)
                nc.scalar.activation(gate[:, 1:2], gate[:, 0:1], ACT.Tanh).then_inc(sem["gate_done"], 1)
            for j, (_, _, w, n, scale) in enumerate(wunits):
                if scale is None:
                    act.wait_ge(sem["gate_done"], 1)
                if W_T:
                    act.wait_ge(sem["wT_mm"], j + 1)
                    src, dst = ps[:, 4:8, :], w[:, HI]
                else:
                    act.wait_ge(sem[f"w_in{j % 2}"], 16 * (j // 2 + 1))
                    src, dst = stage_of(j, n), w[:, HI]
                if scale is None:
                    nc.scalar.activation(dst, src, ACT.Identity, scale=gate[:, 1:2]).then_inc(sem["w_hi"], 1)
                else:
                    nc.scalar.activation(dst, src, ACT.Copy, scale=scale).then_inc(sem["w_hi"], 1)

            def high(v, u, kind, dst):
                for t in range(TT):
                    act.wait_ge(sem["pe_T"], item_no(v, u, (kind, t)) + 1)
                    nc.scalar.activation(dst[:, HI, :, t * P:(t + 1) * P],
                                         ps[:, T_BANK[kind, t], :].rearrange("p (k s) -> p k s", k=KC),
                                         ACT.Copy).then_inc(sem["act_hi"], 1)

            high(-1, 0, "x", xT)
            high(-1, 0, "c", cT)

            def body(v, vf, vb, vo, u):
                F, B, O, N = front(v), back(v), outp(v), nxt(v)
                for g in range(STEPS):
                    sa = back_step(vf, vb, g, 2)
                    sp_ = back_step(vf, vb, g, 3)
                    for p in range(NPAIR):
                        if F and p == NPAIR - 1:
                            high_qk(vf, g)
                        if B and p == NPAIR - 1:
                            act.wait_ge(sem["pe_pv"], (vb * STEPS + g) + 1)
                            if g:
                                act.wait_ge(sem["pe_T"], item_no(v, u, ("BT", g - 1)) + 1)
                            nc.scalar.activation(OTs[:, 0:L["ot"]], ps[:, B_OT, 0:L["ot"]], ACT.Copy).then_inc(sem["act_ot"], 1)
                        if sp_ is not None:
                            n = unit(sp_[0], sp_[1], 2 * p)
                            act.wait_ge(sem["pe_pt"], n + 1)
                            nc.scalar.activation(PTb[:, sp_[1] % 2, 0, 2 * p:2 * p + 2, :],
                                                 ps[:, B_PT, :].rearrange("p (h s) -> p h s", h=2),
                                                 ACT.Copy).then_inc(sem["act_pt"], 1)
                        if O and g == 0 and p == 0:
                            high(v, u, "y", yT)
                        if sa is not None:
                            for t in range(TT):
                                n = unit(sa[0], sa[1], 2 * p + t)
                                act.wait_ge(sem["dve_max"], n + 1)
                                for h in (2 * p, 2 * p + 1):
                                    if GQA:
                                        last = nc.scalar.activation(Pb[:, t, h], Pb[:, t, h], ACT.Exp, bias=negmax[:, t, h:h + 1],
                                                                    scale=-1.0)
                                    else:
                                        last = nc.scalar.activation(
                                            Pb[:, t, h], ps[:, B_A + t, (h % 2) * S:(h % 2 + 1) * S], ACT.Exp,
                                            bias=negmax[:, t, h:h + 1], accum_out=sums[:, sa[1], t, h:h + 1])
                                last.then_inc(sem["act_exp"], 1)
                if N:
                    high(v, u, "x", xT)
                    high(v, u, "c", cT)

            def high_qk(vf, g):
                act.wait_ge(sem["pe_qk"], (vf * STEPS + g) + 1)
                wait(act, e_written[g % 2], (vf * 2 + g // 2) * 16)
                kcol = None if L["kcol"] is None else L["kcol"] + (0 if GQA else g)
                kbias = None if kcol is None else c["cols"][:, kcol:kcol + 1]
                qbias = None if L["qcol"] is None else c["cols"][:, L["qcol"] + g:L["qcol"] + g + 1]
                if GQA:
                    if g == 0:
                        wait(act, sem["ek_w"], vf * 16)
                        nc.scalar.activation(EK[:, 0], ps[:, B_QK, S:2 * S], ACT.Identity, bias=kbias)
                    nc.scalar.activation(E[:, g % 2, 0], ps[:, B_QK, 0:S], ACT.Identity, bias=qbias).then_inc(sem["act_e"], 1)
                elif qbias is None:
                    nc.scalar.activation(E[:, g % 2, 0:4:3, :], ps[:, B_QK, :].rearrange("p (j s) -> p j s", j=2),
                                         ACT.Copy).then_inc(sem["act_e"], 1)
                else:
                    nc.scalar.activation(E[:, g % 2, 0], ps[:, B_QK, 0:S], ACT.Identity, bias=qbias)
                    nc.scalar.activation(E[:, g % 2, 3], ps[:, B_QK, S:2 * S], ACT.Identity, bias=kbias).then_inc(sem["act_e"], 1)

            bodies(act, body)

        @block.vector
        def _(dve):
            def stats_of(src, sm, n, tiles_stats, tiles_mv, bs, mvs, ready):
                for t in range(TT):
                    ready(t)
                    nc.vector.bn_stats(tiles_stats[:, t], src[:, t]).then_inc(sem[bs], 1)
                dve.wait_ge(sem[bs], n * TT + TT)
                nc.vector.memset(dummy[:, UNITS:UNITS + 1], 0.0)
                for t in range(TT):
                    nc.vector.bn_aggr(tiles_mv[:, t], tiles_stats[:, t]).then_inc(sem[mvs], 1)

            lsrc = xin if ln_x else cin

            def norm_stats(n):
                stats_of(lsrc, None, n, stats, mv, "dve_bs", "dve_mv",
                         lambda t: dve.wait_ge(sem["x_in" if ln_x else "c_in"], n * 16 + 16) if t == 0 else None)

            def norm_apply(n):
                dve.wait_ge(sem["pool_rs"], n + 1)
                for t in range(TT):
                    nc.vector.tensor_scalar(norm[:, t], lsrc[:, t], mv[:, t, 0:1], rstd[:, t:t + 1],
                                            ALU.subtract, ALU.mult).then_inc(sem["dve_xn"], 1)

            if has_ln:
                norm_stats(0)
                norm_apply(0)
            for j, (_, _, w, n, scale) in enumerate(wunits):
                dve.wait_ge(sem["w_hi"], j + 1)
                src = ps[:, 4:8, :] if W_T else stage_of(j, n)
                for k in range(KC):
                    last = nc.vector.scalar_tensor_tensor(w[:, LO, k], src[:, k], gate[:, 1:2] if scale is None else scale,
                                                          w[:, HI, k], ALU.mult, ALU.subtract)
                last.then_inc(sem["w_lo"], 1)

            def low(v, u, kind, dst):
                for t in range(TT):
                    dve.wait_ge(sem["act_hi"], turn_no(v, u, (kind, t)) + 1)
                    nc.vector.tensor_tensor(dst[:, LO, :, t * P:(t + 1) * P],
                                            ps[:, T_BANK[kind, t], :].rearrange("p (k s) -> p k s", k=KC),
                                            dst[:, HI, :, t * P:(t + 1) * P], ALU.subtract).then_inc(sem["dve_T"], 1)

            low(-1, 0, "x", xT)
            low(-1, 0, "c", cT)
            if "vb" in rows or "ob" in rows:
                dve.wait_ge(sem["row_in"], 16 * len(L["rows"]))
            dve.wait_ge(sem["ones_done"], 1)

            def body(v, vf, vb, vo, u):
                F, B, O, N = front(v), back(v), outp(v), nxt(v)
                for g in range(STEPS):
                    if has_ln and N and g == 1:
                        norm_stats(vf + 1)
                    if has_ln and N and g == 2:
                        dve.wait_ge(sem["pe_T"], ahead(v, u))
                        norm_apply(vf + 1)
                    sa = back_step(vf, vb, g, 2)
                    sp_ = back_step(vf, vb, g, 3)
                    for p in range(NPAIR):
                        if sp_ is not None:
                            n = unit(sp_[0], sp_[1], 2 * p + 1)
                            dve.wait_ge(sem["pe_pt"], n + 1)
                            nc.vector.tensor_copy(PTb[:, sp_[1] % 2, 1, 2 * p:2 * p + 2, :],
                                                  ps[:, B_PT + 1, :].rearrange("p (h s) -> p h s", h=2)).then_inc(sem["dve_pt"], 1)
                        if F and p == NPAIR - 1:
                            low_qk(vf, g)
                        if O and g == 0 and p == 0:
                            low(v, u, "y", yT)
                        if sa is not None:
                            for t in range(TT):
                                n = unit(sa[0], sa[1], 2 * p + t)
                                if GQA and sa[1] == 0 and p == 0 and t == 0:
                                    dve.wait_ge(sem["mask_in"], sa[0] * 16 + 16)
                                    nc.vector.tensor_copy(maskN[:], mask_next[:]).then_inc(sem["dve_mask"], 1)
                                    dve.wait_ge(sem["dve_mask"], sa[0] + 1)
                                dve.wait_ge(sem["pe_a"], n + 1)
                                if GQA:
                                    nc.vector.memset(dummy[:, 2 * p + t:2 * p + t + 1], 0.0)
                                    for h in (2 * p, 2 * p + 1):
                                        last = nc.vector.tensor_tensor_reduce(
                                            Pb[:, t, h], ps[:, B_A + t, (h % 2) * S:(h % 2 + 1) * S], maskN[:, t, :],
                                            -1.0, 3.0e38, ALU.add, ALU.min, negmax[:, t, h:h + 1])
                                    last.then_inc(sem["dve_max"], 1)
                                else:
                                    nc.vector.tensor_reduce(negmax[:, t, 2 * p:2 * p + 2],
                                                            ps[:, B_A + t, :].rearrange("p (h s) -> p h s", h=2),
                                                            AX_X, ALU.max, negate=True).then_inc(sem["dve_max"], 1)
                    if O and g in (1, 2):
                        add_output(v, u, vo, g - 1)
                    if F and g == 3:
                        values(v, u, 0)
                    if B and g < 3:
                        divide(v, u, vb, g)
                if O and post_ln:
                    stats_of(xres, None, vo, pstats, pmv, "dve_pbs", "dve_pmv",
                             lambda t: dve.wait_ge(sem["dve_T"], item_no(v, u, ("O", 1)) + 1) if t == 0 else None)
                if N:
                    low(v, u, "x", xT)
                if F:
                    values(v, u, 1)
                if B:
                    divide(v, u, vb, 3)
                if N:
                    low(v, u, "c", cT)
                if O and post_ln:
                    wait(dve, sem["out_st"], vo * 16)
                    dve.wait_ge(sem["pool_prs"], vo + 1)
                    for t in range(TT):
                        nc.vector.tensor_scalar(xo[:, t], xres[:, t], pmv[:, t, 0:1], prstd[:, t:t + 1],
                                                ALU.subtract, ALU.mult).then_inc(sem["dve_pxn"], 1)

            def values(v, u, t):
                dve.wait_ge(sem["pe_T"], item_no(v, u, ("V", t)) + 1)
                bank = ps[:, T_BANK["V", t], :]
                if GQA:
                    nc.vector.tensor_tensor(V[:, t, :, 0:HD], bank[:, 0:NK].rearrange("p (h d) -> p h d", d=HD),
                                            rows["vb"][:].rearrange("p (h d) -> p h d", d=HD), ALU.add).then_inc(sem["dve_T"], 1)
                elif "vb" in rows:
                    nc.vector.tensor_tensor(V[:, t], bank, rows["vb"][:], ALU.add).then_inc(sem["dve_T"], 1)
                else:
                    nc.vector.tensor_copy(V[:, t], bank).then_inc(sem["dve_T"], 1)

            def low_qk(vf, g):
                dve.wait_ge(sem["act_e"], (vf * STEPS + g) + 1)
                if GQA:
                    kb = c["cols"][:, L["kcol"]:L["kcol"] + 1]
                    qb = c["cols"][:, L["qcol"] + g:L["qcol"] + g + 1]
                    if g == 0:
                        nc.vector.scalar_tensor_tensor(EK[:, 1], ps[:, B_QK, S:2 * S], kb, EK[:, 0], ALU.add, ALU.subtract)
                    nc.vector.scalar_tensor_tensor(E[:, g % 2, 1], ps[:, B_QK, 0:S], qb, E[:, g % 2, 0],
                                                   ALU.add, ALU.subtract).then_inc(sem["dve_e"], 1)
                else:
                    for j, (lo_, hi_, col) in enumerate(((2, 0, L["qcol"]), (1, 3, L["kcol"]))):
                        last = nc.vector.scalar_tensor_tensor(
                            E[:, g % 2, lo_], ps[:, B_QK, j * S:(j + 1) * S],
                            0.0 if col is None else c["cols"][:, col + g:col + g + 1], E[:, g % 2, hi_], ALU.add, ALU.subtract)
                    last.then_inc(sem["dve_e"], 1)

            def divide(v, u, vb, g):
                dve.wait_ge(sem["pe_T"], item_no(v, u, ("BT", g)) + 1)
                bank = ps[:, T_BANK["BT", g], :]
                rcp = rcp2[:, g % 2]
                if GQA:
                    o = bank.rearrange("p (u t h d) -> p u t h d", u=2, t=TT, h=4)
                    rc = rcp.rearrange("p (u t h) -> p u t h", u=2, t=TT)
                    nc.vector.reciprocal(rcp.rearrange("p (a h) -> p a h", a=4),
                                         bank.rearrange("p (a h d) -> p a h d", a=4, h=4)[:, :, :, HD]).then_inc(sem["dve_rc"], 1)
                    dve.wait_ge(sem["dve_rc"], (vb * STEPS + g) + 1)
                    for w in range(2):
                        yv = y[:, :, g * P + w * 64:g * P + (w + 1) * 64].rearrange("p t (h d) -> p t h d", h=4)
                        last = nc.vector.tensor_tensor(yv, o[:, w, :, :, 0:HD],
                                                       rc[:, w].unsqueeze(3).broadcast_to([P, TT, 4, HD]), ALU.mult)
                    last.then_inc(sem["dve_T"], 1)
                else:
                    nc.vector.reciprocal(rcp[:, 0:TT * HS], sums[:, g].rearrange("p t h -> p (t h)")).then_inc(sem["dve_rc"], 1)
                    dve.wait_ge(sem["dve_rc"], (vb * STEPS + g) + 1)
                    nc.vector.tensor_tensor(
                        y[:, :, g * P:(g + 1) * P].rearrange("p t (h d) -> p t h d", h=HS),
                        bank[:, 0:TT * P].rearrange("p (t h d) -> p t h d", t=TT, h=HS),
                        rcp[:, 0:TT * HS].rearrange("p (t h) -> p t h", t=TT).unsqueeze(3).broadcast_to([P, TT, HS, HD]),
                        ALU.mult).then_inc(sem["dve_T"], 1)

            def add_output(v, u, vo, t):
                if t == 0:
                    if not post_ln:
                        wait(dve, sem["out_st"], vo * 16)
                    if "ob" in rows:
                        dve.wait_ge(sem["pool_res"], vo * TT + TT)
                    else:
                        dve.wait_ge(sem["xres_in"], vo * 16 + 16)
                dve.wait_ge(sem["pe_T"], item_no(v, u, ("O", t)) + 1)
                nc.vector.tensor_tensor((xres if post_ln else xo)[:, t], ps[:, T_BANK["O", t], :], xres[:, t],
                                        ALU.add).then_inc(sem["dve_T"], 1)

            bodies(dve, body)

        @block.tensor
        def _(pe):
            if W_T:
                for j in range(4):
                    pe.wait_ge(sem[f"w_in{j % 2}"], 16 * (j // 2 + 1))
                    if j:
                        pe.wait_ge(sem["w_lo"], j)
                    src = stage_of(j, D)
                    for k in range(KC):
                        for o in range(KC):
                            last = nc.tensor.transpose(ps[:, 4 + k, o * P:(o + 1) * P], src[:, o, k * P:(k + 1) * P], ident[:])
                    last.then_inc(sem["wT_mm"], 1)

            def bank_free(v, u, key):
                wait(pe, sem["dve_T"], before_in_bank(v, u, key))

            def turn(v, u, kind, src):
                for t in range(TT):
                    bank_free(v, u, (kind, t))
                    for k in range(KC):
                        last = nc.tensor.transpose(ps[:, T_BANK[kind, t], k * P:(k + 1) * P], src[:, t, k * P:(k + 1) * P], ident[:])
                    last.then_inc(sem["pe_T"], 1)

            NM = len(PAIRS) * KC

            def token_product(kind, t, aT, w, width, part=range(NM)):
                for m in part:
                    (a, b), k = PAIRS[m // KC], m % KC
                    last = nc.tensor.matmul(ps[:, T_BANK[kind, t], 0:width], aT[:, a, k, t * P:(t + 1) * P], w[:, b, k, :],
                                            start=(m == 0), stop=(m == NM - 1))
                if part[-1] == NM - 1:
                    last.then_inc(sem["pe_T"], 1)

            def src_ready(is_norm, name, n):
                if is_norm:
                    pe.wait_ge(sem["pool_b"], n * TT + TT)
                else:
                    pe.wait_ge(sem[name], n * 16 + 16)

            src_ready(ln_x, "x_in", 0)
            turn(-1, 0, "x", xsrc)
            src_ready(ln_c, "c_in", 0)
            turn(-1, 0, "c", csrc)
            pe.wait_ge(sem["w_lo"], 4)
            pe.wait_ge(sem["ones_done"], 1)

            def qk_product(g, part, of):
                operands = [(0, wq, xT, g * P)]
                if not GQA or g == 0:
                    operands.append((S, wk, cT, 0 if GQA else g * P))
                n = NM * len(operands)
                for m in range(part * n // of, (part + 1) * n // of):
                    (col0, w, aT, n0), i = operands[m // NM], m % NM
                    (a, h), k = PAIRS[i // KC], i % KC
                    last = nc.tensor.matmul(ps[:, B_QK, col0:col0 + S], w[:, a, k, n0:n0 + P], aT[:, h, k, :],
                                            start=(i == 0), stop=(i == NM - 1))
                if part == of - 1:
                    last.then_inc(sem["pe_qk"], 1)

            def head_outputs(v, u, vb, g, p):
                if p == 0:
                    if g == 0:
                        pe.wait_ge(sem["dve_T"], ahead(v, u) - 2 if nxt(v - 1) else ahead(v, u))
                    pe.wait_ge(sem["act_pt"], (vb * STEPS + g) * NPAIR + NPAIR)
                    pe.wait_ge(sem["dve_pt"], (vb * STEPS + g) * NPAIR + NPAIR)
                    wait(pe, sem["act_ot"], vb * STEPS + g)
                w, kt = p // TT, p % TT
                for j in range(4):
                    if GQA:
                        lhsT = V[:, kt, 2 * g + w, :]
                    else:
                        lhsT = V[:, kt, (4 * g + j) * HD:(4 * g + j + 1) * HD]
                    last = nc.tensor.matmul(ps[32 * j:32 * j + 32, B_OT, w * S:(w + 1) * S], lhsT,
                                            PTb[:, g % 2, kt, 4 * w + j, :], start=(kt == 0), stop=(kt == TT - 1))
                if p == NPAIR - 1:
                    last.then_inc(sem["pe_pv"], 1)

            def body(v, vf, vb, vo, u):
                F, B, O, N = front(v), back(v), outp(v), nxt(v)
                for g in range(STEPS):
                    if F:
                        if g == 0:
                            pe.wait_ge(sem["dve_T"], ahead(v, u) - 2)
                        wait(pe, sem["dve_e"], vf * STEPS + g)

                    sa = back_step(vf, vb, g, 2)
                    sp_ = back_step(vf, vb, g, 3)
                    for p in range(NPAIR):
                        if F:
                            qk_product(g, 2 * p, 2 * NPAIR - 1)
                        if B:
                            head_outputs(v, u, vb, g, p)
                        if sp_ is not None:
                            b, gg = sp_
                            for kt in range(TT):
                                pe.wait_ge(sem["act_exp"], unit(b, gg, 2 * p + 2))
                                wait(pe, sem["act_pt" if kt == 0 else "dve_pt"], (b * STEPS + gg) * NPAIR + p)
                                for hh in range(2):
                                    for t in range(TT):
                                        last = nc.tensor.transpose(ps[:, B_PT + kt, hh * S + t * P:hh * S + (t + 1) * P],
                                                                   Pb[:, t, 2 * p + hh, kt * P:(kt + 1) * P], ident[:])
                                last.then_inc(sem["pe_pt"], 1)
                        if O and g == 0 and p == 0:
                            pe.wait_ge(sem["dve_T"], ahead(v, u) - (2 if nxt(v - 1) else 0))
                            turn(v, u, "y", y)
                        if F and p < NPAIR - 1:
                            if g == 0 and p == 0:
                                pe.wait_ge(sem["dve_T"], ahead(v, u))
                            qk_product(g, 2 * p + 1, 2 * NPAIR - 1)
                        if sa is not None:
                            b, gg = sa
                            if p == 0:
                                pe.wait_ge(stacked[gg], b * (16 * n_reads) + 16 * n_reads)
                            for t in range(TT):
                                wait(pe, sem["dve_max" if GQA else "act_exp"], unit(b, gg, 2 * p + t - 1))
                                for hh in range(2):
                                    h = 2 * p + hh
                                    if GQA:
                                        lhsT, rhs = qst[0:KROWS, gg, h, t * P:(t + 1) * P], kst[0:KROWS, gg, h // 4, :]
                                    else:
                                        lhsT, rhs = st[0:KROWS, gg, h, 0, t * P:(t + 1) * P], st[0:KROWS, gg, h, 1, :]
                                    last = nc.tensor.matmul(ps[:, B_A + t, hh * S:(hh + 1) * S], lhsT, rhs, start=True, stop=True)
                                last.then_inc(sem["pe_a"], 1)
                        part = range(p * NM // NPAIR, (p + 1) * NM // NPAIR)
                        if O and g in (1, 2):
                            if p == 0:
                                pe.wait_ge(sem["dve_T"], item_no(v, u, ("y", g - 1)) + 1)
                                bank_free(v, u, ("O", g - 1))
                            token_product("O", g - 1, yT, wo, D, part)
                        if F and g == 3:
                            if p == 0:
                                bank_free(v, u, ("V", 0))
                            token_product("V", 0, cT, wv, NK, part)
                    if B and g < 3:
                        turn_outputs(v, u, vb, g)
                if F:
                    pe.wait_ge(sem["dve_e"], vf * STEPS + STEPS)
                if N:
                    src_ready(ln_x, "x_in", vf + 1)
                    turn(v, u, "x", xsrc)
                if F:
                    bank_free(v, u, ("V", 1))
                    token_product("V", 1, cT, wv, NK)
                if B:
                    turn_outputs(v, u, vb, 3)
                if N:
                    src_ready(ln_c, "c_in", vf + 1)
                    turn(v, u, "c", csrc)

            def turn_outputs(v, u, vb, g):
                bank_free(v, u, ("BT", g))
                pe.wait_ge(sem["act_ot"], (vb * STEPS + g) + 1)
                for a in range(L["ot"] // P):
                    last = nc.tensor.transpose(ps[:, T_BANK["BT", g], a * P:(a + 1) * P], OTs[:, a * P:(a + 1) * P], ident[:])
                last.then_inc(sem["pe_T"], 1)

            bodies(pe, body)


def mlp_phase(nc, c, A, half, x_ln, x_res, x_out):
    NJ = INNER // 2 // P
    ps, ident = c["ps"], c["ident"]
    B_T, B_O = 4, 6
    with ExitStack() as ctx:
        al = Buffers(nc, ctx, f"mlp{half}")
        w1 = al.sb("w1", [P, 2, KC, NJ * P], F32R)
        w2 = al.sb("w2", [P, 2, NJ, D], F32R)
        stage = [al.sb(f"stage{i}", [P, KC, D]) for i in range(2)]
        xin = al.sb("xin", [P, TT, D])
        norm = al.sb("norm", [P, TT, D])
        xT = al.sb("xT", [P, 2, KC, S], F32R)
        gf = al.sb("gf", [P, 4, 2 * S])
        gT = al.sb("gT", [P, 2, NJ, S], F32R)
        xres = al.sb("xres", [P, TT, D])
        xo = al.sb("xo", [P, TT, D])
        rows = {n: al.sb(f"row_{n}", [P, D]) for n in ("g", "b", "ob")}
        stats, mv = al.sb("stats", [P, TT, 6]), al.sb("mv", [P, TT, 2])
        veps, rstd, eps = (al.sb(n, [P, TT]) for n in ("veps", "rstd", "eps"))
        dummy = al.sb("dummy", [P, 1])
        sem = {n: al.sem(n) for n in ("w_in0 w_in1 row_in x_in xres_in out_st w_hi w_lo pe_x act_x dve_x pe_fc act_g act_gh dve_g "
                                      "pe_o dve_o eps_set dve_bs dve_mv pool_ve pool_rs dve_xn pool_g pool_b pool_res").split()}
        block = ctx.enter_context(nc.Block())
        W1, W2 = A["L0_xattn_fc_w"], A["L0_xattn_proj_w"]
        j0 = half * NJ
        wunits = [(W1[:, (j0 + 4 * i) * P:(j0 + 4 * i + 4) * P].rearrange("(k p) n -> p k n", p=P),
                   [w1[:, hl, :, i * D:(i + 1) * D] for hl in range(2)]) for i in range(2)]
        wunits += [(W2[(j0 + 4 * i) * P:(j0 + 4 * i + 4) * P, :].rearrange("(k p) n -> p k n", p=P),
                    [w2[:, hl, 4 * i:4 * i + 4, :] for hl in range(2)]) for i in range(2)]
        fcb = c["col"]["L0_xattn_fc_b"] + j0

        def bodies(eng, body):
            with eng.Fori(0, NB - 1) as v:
                body(v, True)
            body(NB - 1, False)

        @block.sync
        def _(sp):
            sp.dma_start(xin[:], rows_of(x_ln, 0)).then_inc(sem["x_in"], 16)
            for n, src in (("g", "L0_xattn_ln2_w"), ("b", "L0_xattn_ln2_b"), ("ob", "L0_xattn_proj_b")):
                sp.dma_start(rows[n][:], A[src].partition_broadcast(P)).then_inc(sem["row_in"], 16)
            for j, (src, _) in enumerate(wunits):
                if j >= 2:
                    sp.wait_ge(sem["w_lo"], j - 1)
                sp.dma_start(stage[j % 2][:], src).then_inc(sem[f"w_in{j % 2}"], 16)

            def body(v, N):
                if N:
                    sp.wait_ge(sem["dve_xn"], v * TT + TT)
                    sp.dma_start(xin[:], rows_of(x_ln, v + 1)).then_inc(sem["x_in"], 16)
                wait(sp, sem["dve_o"], v * TT)
                sp.dma_start(xres[:], rows_of(x_res, v)).then_inc(sem["xres_in"], 16)
                sp.wait_ge(sem["dve_o"], v * TT + TT)
                sp.dma_start(rows_of(x_out, v), xo[:]).then_inc(sem["out_st"], 16)

            bodies(sp, body)
            sp.wait_ge(sem["out_st"], 16 * NB)

        @block.gpsimd
        def _(pool):
            nc.gpsimd.memset(eps[:], 1e-5).then_inc(sem["eps_set"], 1)
            pool.wait_ge(sem["eps_set"], 1)
            pool.wait_ge(sem["row_in"], 48)

            def norm_rows(n):
                pool.wait_ge(sem["dve_mv"], n * TT + TT)
                nc.gpsimd.tensor_tensor(veps[:], mv[:, :, 1], eps[:], ALU.add).then_inc(sem["pool_ve"], 1)
                pool.wait_ge(sem["pool_ve"], n + 1)
                nc.gpsimd.tensor_tensor(rstd[:], veps[:], c["half"][:, 0:TT], ALU.pow).then_inc(sem["pool_rs"], 1)
                for t in range(TT):
                    pool.wait_ge(sem["dve_xn"], n * TT + (t + 1))
                    nc.gpsimd.tensor_tensor(norm[:, t], norm[:, t], rows["g"][:], ALU.mult).then_inc(sem["pool_g"], 1)
                    pool.wait_ge(sem["pool_g"], n * TT + (t + 1))
                    nc.gpsimd.tensor_tensor(norm[:, t], norm[:, t], rows["b"][:], ALU.add).then_inc(sem["pool_b"], 1)

            norm_rows(0)

            def body(v, N):
                if half == 0:
                    pool.wait_ge(sem["xres_in"], v * 16 + 16)
                    for t in range(TT):
                        nc.gpsimd.tensor_tensor(xres[:, t], xres[:, t], rows["ob"][:], ALU.add).then_inc(sem["pool_res"], 1)
                if N:
                    norm_rows(v + 1)

            bodies(pool, body)

        @block.scalar
        def _(act):
            for j, (_, dst) in enumerate(wunits):
                act.wait_ge(sem[f"w_in{j % 2}"], 16 * (j // 2 + 1))
                nc.scalar.activation(dst[HI], stage[j % 2][:], ACT.Copy).then_inc(sem["w_hi"], 1)

            def high(n, t):
                act.wait_ge(sem["pe_x"], n * TT + (t + 1))
                nc.scalar.activation(xT[:, HI, :, t * P:(t + 1) * P], ps[:, B_T + t, :].rearrange("p (k s) -> p k s", k=KC),
                                     ACT.Copy).then_inc(sem["act_x"], 1)

            for t in range(TT):
                high(0, t)

            def body(v, N):
                for q in range(NJ // 2):
                    act.wait_ge(sem["pe_fc"], v * (NJ // 2) + (q + 1))
                    for i in range(2):
                        last = nc.scalar.activation(gf[:, q, i * S:(i + 1) * S], ps[:, q, i * S:(i + 1) * S], ACT.Gelu_apprx_tanh,
                                                    bias=c["cols"][:, fcb + 2 * q + i:fcb + 2 * q + i + 1])
                    last.then_inc(sem["act_g"], 1)
                    act.wait_ge(sem["act_g"], v * (NJ // 2) + (q + 1))
                    nc.scalar.activation(gT[:, HI, 2 * q:2 * q + 2, :], gf[:, q].rearrange("p (j s) -> p j s", j=2),
                                         ACT.Copy).then_inc(sem["act_gh"], 1)
                if N:
                    for t in range(TT):
                        high(v + 1, t)

            bodies(act, body)

        @block.vector
        def _(dve):
            def norm_stats(n):
                dve.wait_ge(sem["x_in"], n * 16 + 16)
                for t in range(TT):
                    nc.vector.bn_stats(stats[:, t], xin[:, t]).then_inc(sem["dve_bs"], 1)
                dve.wait_ge(sem["dve_bs"], n * TT + TT)
                nc.vector.memset(dummy[:], 0.0)
                for t in range(TT):
                    nc.vector.bn_aggr(mv[:, t], stats[:, t]).then_inc(sem["dve_mv"], 1)

            def norm_apply(n):
                dve.wait_ge(sem["pool_rs"], n + 1)
                wait(dve, sem["pe_x"], n * TT)
                for t in range(TT):
                    nc.vector.tensor_scalar(norm[:, t], xin[:, t], mv[:, t, 0:1], rstd[:, t:t + 1],
                                            ALU.subtract, ALU.mult).then_inc(sem["dve_xn"], 1)

            norm_stats(0)
            norm_apply(0)
            for j, (_, dst) in enumerate(wunits):
                dve.wait_ge(sem["w_hi"], j + 1)
                nc.vector.tensor_tensor(dst[LO], stage[j % 2][:], dst[HI], ALU.subtract).then_inc(sem["w_lo"], 1)

            def low(n, t):
                dve.wait_ge(sem["act_x"], n * TT + (t + 1))
                nc.vector.tensor_tensor(xT[:, LO, :, t * P:(t + 1) * P], ps[:, B_T + t, :].rearrange("p (k s) -> p k s", k=KC),
                                        xT[:, HI, :, t * P:(t + 1) * P], ALU.subtract).then_inc(sem["dve_x"], 1)

            for t in range(TT):
                low(0, t)

            def body(v, N):
                for q in range(NJ // 2):
                    if N and q == 1:
                        norm_stats(v + 1)
                    if N and q == 2:
                        norm_apply(v + 1)
                    dve.wait_ge(sem["act_gh"], v * (NJ // 2) + (q + 1))
                    nc.vector.tensor_tensor(gT[:, LO, 2 * q:2 * q + 2, :], gf[:, q].rearrange("p (j s) -> p j s", j=2),
                                            gT[:, HI, 2 * q:2 * q + 2, :], ALU.subtract).then_inc(sem["dve_g"], 1)
                if N:
                    for t in range(TT):
                        low(v + 1, t)
                wait(dve, sem["out_st"], v * 16)
                if half == 0:
                    dve.wait_ge(sem["pool_res"], v * TT + TT)
                else:
                    dve.wait_ge(sem["xres_in"], v * 16 + 16)
                for t in range(TT):
                    dve.wait_ge(sem["pe_o"], v * TT + (t + 1))
                    nc.vector.tensor_tensor(xo[:, t], ps[:, B_O + t, :], xres[:, t], ALU.add).then_inc(sem["dve_o"], 1)

            bodies(dve, body)

        @block.tensor
        def _(pe):
            def turn(n, t):
                for k in range(KC):
                    last = nc.tensor.transpose(ps[:, B_T + t, k * P:(k + 1) * P], norm[:, t, k * P:(k + 1) * P], ident[:])
                last.then_inc(sem["pe_x"], 1)

            pe.wait_ge(sem["pool_b"], TT)
            for t in range(TT):
                turn(0, t)
            pe.wait_ge(sem["w_lo"], 4)

            def body(v, N):
                pe.wait_ge(sem["dve_x"], v * TT + TT)
                for q in range(NJ // 2):
                    for i in range(2):
                        j = 2 * q + i
                        for a, (wa, xa) in enumerate(PAIRS):
                            for k in range(KC):
                                last = nc.tensor.matmul(ps[:, q, i * S:(i + 1) * S], w1[:, wa, k, j * P:(j + 1) * P], xT[:, xa, k, :],
                                                        start=(a == 0 and k == 0), stop=(a == 2 and k == KC - 1))
                    last.then_inc(sem["pe_fc"], 1)
                if N:
                    pe.wait_ge(sem["pool_b"], v * TT + 2 * TT)
                    for t in range(TT):
                        turn(v + 1, t)
                wait(pe, sem["dve_o"], v * TT)
                for t in range(TT):
                    for j in range(NJ):
                        if t == 0 and j % 2 == 0:
                            pe.wait_ge(sem["dve_g"], v * (NJ // 2) + (j // 2 + 1))
                        for a, (ga, wa) in enumerate(PAIRS):
                            last = nc.tensor.matmul(ps[:, B_O + t, :], gT[:, ga, j, t * P:(t + 1) * P], w2[:, wa, j, :],
                                                    start=(a == 0 and j == 0), stop=(a == 2 and j == NJ - 1))
                    last.then_inc(sem["pe_o"], 1)

            bodies(pe, body)


def single_head_phase(nc, c, A, x_in, x_out):
    ps, ident = c["ps"], c["ident"]
    B_G, B_V, B_S, B_PT, B_O, B_T = 0, 2, 4, 5, 6, 7
    with ExitStack() as ctx:
        al = Buffers(nc, ctx, "l1")
        raw = {n: al.sb(f"raw_{n}", [P, KC, D]) for n in "qkvo"}
        woT = al.sb("woT", [P, KC, D])
        a1 = al.sb("a1", [P, 2, KC, D], F32R)
        a2 = al.sb("a2", [P, 2, KC, D], F32R)
        xin, cin = al.sb("xin", [P, TT, D]), al.sb("cin", [P, TT, D])
        xT, cT = al.sb("xT", [P, 2, KC, S], F32R), al.sb("cT", [P, 2, KC, S], F32R)
        G = al.sb("G", [P, 2, KC, S], F32R)
        VO = al.sb("VO", [P, 2, TT, D], F32R)
        Pb = al.sb("Pb", [P, TT, S])
        PT = al.sb("PT", [P, 2, TT, S], F32R)
        xres, xo = al.sb("xres", [P, TT, D]), al.sb("xo", [P, TT, D])
        alpha = al.sb("alpha", [P, 1])
        negmax, sums, rcp, fac = (al.sb(n, [P, TT]) for n in ("negmax", "sums", "rcp", "fac"))
        sem = {n: al.sem(n) for n in ("w_in al_in x_in c_in xres_in out_st pe_wt act_wt pe_a act_a dve_a pe_T act_T dve_T pe_G act_G "
                                      "dve_G pe_V act_V dve_V pe_S dve_max act_exp pe_PT act_PT dve_PT pe_O dve_O dve_rc dve_fac").split()}
        block = ctx.enter_context(nc.Block())
        names = {"q": "L1_xattn_w_q", "k": "L1_xattn_w_k", "v": "L1_xattn_w_v", "o": "L1_xattn_w_o"}

        def bodies(eng, body):
            body(0, -1, True, False, True)
            with eng.Fori(0, NB - 2) as u:
                body(u + 1, u, True, True, True)
            body(NB - 1, NB - 2, True, True, False)
            body(NB, NB - 1, False, True, False)

        @block.sync
        def _(sp):
            for n in "kqov":
                sp.dma_start(raw[n][:], A[names[n]].rearrange("(k p) n -> p k n", p=P)).then_inc(sem["w_in"], 16)
            sp.dma_start(alpha[:], A["L1_xattn_alpha"].partition_broadcast(P)).then_inc(sem["al_in"], 16)
            sp.dma_start(xin[:], rows_of(x_in, 0)).then_inc(sem["x_in"], 16)
            sp.dma_start(cin[:], rows_of(A["ctx_2048"], 0)).then_inc(sem["c_in"], 16)

            def body(vf, vb, F, B, N):
                if N:
                    sp.wait_ge(sem["pe_T"], vf * (2 * TT) + 2 * TT)
                    sp.dma_start(xin[:], rows_of(x_in, vf + 1)).then_inc(sem["x_in"], 16)
                    sp.dma_start(cin[:], rows_of(A["ctx_2048"], vf + 1)).then_inc(sem["c_in"], 16)
                if B:
                    wait(sp, sem["dve_O"], vb * TT)
                    sp.dma_start(xres[:], rows_of(x_in, vb)).then_inc(sem["xres_in"], 16)
                    sp.wait_ge(sem["dve_O"], vb * TT + TT)
                    sp.dma_start(rows_of(x_out, vb), xo[:]).then_inc(sem["out_st"], 16)

            bodies(sp, body)
            sp.wait_ge(sem["out_st"], 16 * NB)

        @block.scalar
        def _(act):
            for k in range(KC):
                act.wait_ge(sem["pe_wt"], k + 1)
                nc.scalar.activation(woT[:, k], ps[:, 4 + k, :], ACT.Copy).then_inc(sem["act_wt"], 1)
            for i, (dst, scale) in enumerate(((a1, D ** -0.5), (a2, 1.0))):
                for k in range(KC):
                    act.wait_ge(sem["pe_a"], i * KC + k + 1)
                    nc.scalar.activation(dst[:, HI, k], ps[:, k, :], ACT.Copy, scale=scale).then_inc(sem["act_a"], 1)

            def high(n, which, dst, t):
                act.wait_ge(sem["pe_T"], n * (2 * TT) + (which * TT + t + 1))
                nc.scalar.activation(dst[:, HI, :, t * P:(t + 1) * P], ps[:, B_T, :].rearrange("p (k s) -> p k s", k=KC),
                                     ACT.Copy).then_inc(sem["act_T"], 1)

            for which, dst in ((0, cT), (1, xT)):
                for t in range(TT):
                    high(0, which, dst, t)

            def body(vf, vb, F, B, N):
                for i in range(2):
                    if F:
                        act.wait_ge(sem["pe_G"], vf * 2 + (i + 1))
                        nc.scalar.activation(G[:, HI, 2 * i:2 * i + 2], ps[:, B_G + i, :].rearrange("p (k s) -> p k s", k=2),
                                             ACT.Copy).then_inc(sem["act_G"], 1)
                    if B and i == 0:
                        act.wait_ge(sem["pe_PT"], vb + 1)
                        nc.scalar.activation(PT[:, HI], ps[:, B_PT, :].rearrange("p (k s) -> p k s", k=TT),
                                             ACT.Copy).then_inc(sem["act_PT"], 1)
                if F:
                    for t in range(TT):
                        act.wait_ge(sem["pe_V"], vf * TT + (t + 1))
                        nc.scalar.activation(VO[:, HI, t], ps[:, B_V + t, :], ACT.Copy).then_inc(sem["act_V"], 1)
                if N:
                    for t in range(TT):
                        high(vf + 1, 0, cT, t)
                if F:
                    act.wait_ge(sem["dve_max"], vf + 1)
                    for t in range(TT):
                        last = nc.scalar.activation(Pb[:, t], ps[:, B_S, t * S:(t + 1) * S], ACT.Exp, bias=negmax[:, t:t + 1],
                                                    accum_out=sums[:, t:t + 1])
                    last.then_inc(sem["act_exp"], 1)
                if N:
                    for t in range(TT):
                        high(vf + 1, 1, xT, t)

            bodies(act, body)

        @block.vector
        def _(dve):
            for i, (dst, scale) in enumerate(((a1, D ** -0.5), (a2, 1.0))):
                for k in range(KC):
                    dve.wait_ge(sem["act_a"], i * KC + k + 1)
                    nc.vector.scalar_tensor_tensor(dst[:, LO, k], ps[:, k, :], scale, dst[:, HI, k],
                                                   ALU.mult, ALU.subtract).then_inc(sem["dve_a"], 1)

            def low(n, which, dst, t):
                dve.wait_ge(sem["act_T"], n * (2 * TT) + (which * TT + t + 1))
                nc.vector.tensor_tensor(dst[:, LO, :, t * P:(t + 1) * P], ps[:, B_T, :].rearrange("p (k s) -> p k s", k=KC),
                                        dst[:, HI, :, t * P:(t + 1) * P], ALU.subtract).then_inc(sem["dve_T"], 1)

            for which, dst in ((0, cT), (1, xT)):
                for t in range(TT):
                    low(0, which, dst, t)
            dve.wait_ge(sem["al_in"], 16)

            def body(vf, vb, F, B, N):
                for i in range(2):
                    if F:
                        dve.wait_ge(sem["act_G"], vf * 2 + (i + 1))
                        nc.vector.tensor_tensor(G[:, LO, 2 * i:2 * i + 2], ps[:, B_G + i, :].rearrange("p (k s) -> p k s", k=2),
                                                G[:, HI, 2 * i:2 * i + 2], ALU.subtract).then_inc(sem["dve_G"], 1)
                    if B and i == 0:
                        dve.wait_ge(sem["act_PT"], vb + 1)
                        nc.vector.tensor_tensor(PT[:, LO], ps[:, B_PT, :].rearrange("p (k s) -> p k s", k=TT),
                                                PT[:, HI], ALU.subtract).then_inc(sem["dve_PT"], 1)
                        nc.vector.reciprocal(rcp[:], sums[:]).then_inc(sem["dve_rc"], 1)
                if B:
                    dve.wait_ge(sem["dve_rc"], vb + 1)
                    nc.vector.tensor_scalar(fac[:], rcp[:], alpha[:, 0:1], None, ALU.mult).then_inc(sem["dve_fac"], 1)
                    dve.wait_ge(sem["dve_fac"], vb + 1)
                    dve.wait_ge(sem["xres_in"], vb * 16 + 16)
                    wait(dve, sem["out_st"], vb * 16)
                    for t in range(TT):
                        dve.wait_ge(sem["pe_O"], vb * TT + (t + 1))
                        nc.vector.scalar_tensor_tensor(xo[:, t], ps[:, B_O, :], fac[:, t:t + 1], xres[:, t],
                                                       ALU.mult, ALU.add).then_inc(sem["dve_O"], 1)
                if F:
                    for t in range(TT):
                        dve.wait_ge(sem["act_V"], vf * TT + (t + 1))
                        nc.vector.tensor_tensor(VO[:, LO, t], ps[:, B_V + t, :], VO[:, HI, t], ALU.subtract).then_inc(sem["dve_V"], 1)
                if N:
                    for t in range(TT):
                        low(vf + 1, 0, cT, t)
                if F:
                    dve.wait_ge(sem["pe_S"], vf + 1)
                    nc.vector.tensor_reduce(negmax[:], ps[:, B_S, :].rearrange("p (t s) -> p t s", t=TT), AX_X, ALU.max,
                                            negate=True).then_inc(sem["dve_max"], 1)
                if N:
                    for t in range(TT):
                        low(vf + 1, 1, xT, t)

            bodies(dve, body)

        @block.tensor
        def _(pe):
            pe.wait_ge(sem["w_in"], 64)
            for k in range(KC):
                for o in range(KC):
                    last = nc.tensor.transpose(ps[:, 4 + k, o * P:(o + 1) * P], raw["o"][:, o, k * P:(k + 1) * P], ident[:])
                last.then_inc(sem["pe_wt"], 1)
            for i, (l, r) in enumerate((("k", raw["q"]), ("v", woT))):
                if i:
                    pe.wait_ge(sem["act_wt"], KC)
                for j in range(KC):
                    if i:
                        pe.wait_ge(sem["dve_a"], j + 1)
                    for o in range(KC):
                        last = nc.tensor.matmul(ps[:, j, :], raw[l][:, o, j * P:(j + 1) * P], r[:, o, :], start=(o == 0), stop=(o == KC - 1))
                    last.then_inc(sem["pe_a"], 1)

            def turn(n, which, src, t):
                wait(pe, sem["dve_T"], n * (2 * TT) + (which * TT + t))
                for k in range(KC):
                    last = nc.tensor.transpose(ps[:, B_T, k * P:(k + 1) * P], src[:, t, k * P:(k + 1) * P], ident[:])
                last.then_inc(sem["pe_T"], 1)

            def turn_all(n, which):
                pe.wait_ge(sem["x_in" if which else "c_in"], n * 16 + 16)
                for t in range(TT):
                    turn(n, which, xin if which else cin, t)

            pe.wait_ge(sem["act_wt"], KC)
            turn_all(0, 0)
            turn_all(0, 1)
            pe.wait_ge(sem["dve_a"], 2 * KC)

            def body(vf, vb, F, B, N):
                if F:
                    pe.wait_ge(sem["dve_T"], vf * (2 * TT) + TT)
                for i in range(2):
                    if F:
                        if B:
                            pe.wait_ge(sem["dve_G"], vb * 2 + (i + 1))
                        for k2 in range(2):
                            m = 2 * i + k2
                            for a, (wa, ca) in enumerate(PAIRS):
                                for k in range(KC):
                                    last = nc.tensor.matmul(ps[:, B_G + i, k2 * S:(k2 + 1) * S], a1[:, wa, k, m * P:(m + 1) * P],
                                                            cT[:, ca, k, :], start=(a == 0 and k == 0), stop=(a == 2 and k == KC - 1))
                        last.then_inc(sem["pe_G"], 1)
                    if B and i == 0:
                        pe.wait_ge(sem["act_exp"], vb + 1)
                        wait(pe, sem["dve_PT"], vb)
                        for kt in range(TT):
                            for t in range(TT):
                                last = nc.tensor.transpose(ps[:, B_PT, kt * S + t * P:kt * S + (t + 1) * P],
                                                           Pb[:, t, kt * P:(kt + 1) * P], ident[:])
                        last.then_inc(sem["pe_PT"], 1)
                if B:
                    pe.wait_ge(sem["dve_PT"], vb + 1)
                    pe.wait_ge(sem["dve_V"], vb * TT + TT)
                    for t in range(TT):
                        wait(pe, sem["dve_O"], vb * TT + t)
                        for a, (pa, va) in enumerate(PAIRS):
                            for kt in range(TT):
                                last = nc.tensor.matmul(ps[:, B_O, :], PT[:, pa, kt, t * P:(t + 1) * P], VO[:, va, kt, :],
                                                        start=(a == 0 and kt == 0), stop=(a == 2 and kt == TT - 1))
                        last.then_inc(sem["pe_O"], 1)
                if F:
                    for t in range(TT):
                        if B:
                            pe.wait_ge(sem["dve_V"], vb * TT + (t + 1))
                        for a, (ca, wa) in enumerate(PAIRS):
                            for k in range(KC):
                                last = nc.tensor.matmul(ps[:, B_V + t, :], cT[:, ca, k, t * P:(t + 1) * P], a2[:, wa, k, :],
                                                        start=(a == 0 and k == 0), stop=(a == 2 and k == KC - 1))
                        last.then_inc(sem["pe_V"], 1)
                if N:
                    turn_all(vf + 1, 0)
                if F:
                    pe.wait_ge(sem["dve_G"], vf * 2 + 2)
                    pe.wait_ge(sem["dve_T"], vf * (2 * TT) + 2 * TT)
                    wait(pe, sem["act_exp"], vf)
                    for t in range(TT):
                        for a, (xa, ga) in enumerate(PAIRS):
                            for k in range(KC):
                                last = nc.tensor.matmul(ps[:, B_S, t * S:(t + 1) * S], xT[:, xa, k, t * P:(t + 1) * P], G[:, ga, k, :],
                                                        start=(a == 0 and k == 0), stop=(a == 2 and k == KC - 1))
                    last.then_inc(sem["pe_S"], 1)
                if N:
                    turn_all(vf + 1, 1)

            bodies(pe, body)


def build(nc, A, out, only=None):
    with ExitStack() as ctx:
        def scratch(name, shape):
            return nc.dram_tensor(name, shape, F32, kind="Internal").ap()

        c = {"col": {}}
        c["ident"] = ctx.enter_context(nc.sbuf_tensor("ident", [P, P], F32))
        c["cols"] = ctx.enter_context(nc.sbuf_tensor("cols", [P, 32], F32))
        c["half"] = ctx.enter_context(nc.sbuf_tensor("half", [P, 8], F32))
        c["ps"] = ctx.enter_context(nc.psum_tensor("ps", [P, 8, BANK], F32))
        c["mask_min"] = scratch("mask_min", (NB, 4 * S))
        c["mask_inf"] = scratch("mask_inf", (NB, 4 * S))
        c["scr"] = [scratch(f"split{g}", (P, 4, S)) for g in range(STEPS)]
        c["scrk"] = scratch("split_k", (P, 2, S))
        hid = [scratch(f"hidden{i}", (NB * S, D)) for i in range(5)]

        setup_phase(nc, c, A)

        mha = {"heads": 16, "hd": 32, "gqa": False, "nk": D, "ot": S, "post_ln": False, "eps": 1e-5, "qscale": 32.0 ** -0.5}
        l0 = ({
            **mha, "tag": "l0", "x_in": A["x"], "x_out": hid[0], "transposed": False, "ln_x": True, "ln_c": False, "oscale": 1.0,
            "wq": "L0_xattn_q_w", "wk": "L0_xattn_k_w", "wv": "L0_xattn_v_w", "wo": "L0_xattn_cproj_w", "mask": c["mask_min"],
            "qcol": c["col"]["L0_xattn_q_b"], "kcol": c["col"]["L0_xattn_k_b"],
            "rows": [("g", "L0_xattn_ln1_w", D), ("b", "L0_xattn_ln1_b", D), ("vb", "L0_xattn_v_b", D), ("ob", "L0_xattn_cproj_b", D)]})
        l2 = ({
            "tag": "l2", "heads": 32, "hd": 16, "gqa": True, "nk": P, "ot": BANK, "post_ln": True, "eps": 1e-6, "qscale": 0.25,
            "x_in": hid[3], "x_out": hid[4], "transposed": False, "ln_x": False, "ln_c": False, "oscale": 1.0,
            "wq": "L2_xattn_Wq", "wk": "L2_xattn_Wk", "wv": "L2_xattn_Wv", "wo": "L2_xattn_Wo",
            "qcol": c["col"]["L2_xattn_bq"], "kcol": c["col"]["L2_xattn_bk"],
            "rows": [("g", "L2_xattn_gamma", D), ("b", "L2_xattn_beta", D), ("vb", "L2_xattn_bv", P), ("ob", "L2_xattn_bo", D)]})
        l3 = ({
            **mha, "tag": "l3", "x_in": hid[4], "x_out": out, "transposed": True, "ln_x": False, "ln_c": True, "oscale": None,
            "wq": "L3_xattn_Wq", "wk": "L3_xattn_Wk", "wv": "L3_xattn_Wv", "wo": "L3_xattn_Wo", "mask": c["mask_inf"],
            "qcol": None, "kcol": None,
            "rows": [("g", "L3_xattn_ln_gamma", D), ("b", "L3_xattn_ln_beta", D)]})
        if only in ("l0", "l2", "l3"):
            L = {"l0": l0, "l2": l2, "l3": l3}[only]
            attention_phase(nc, c, A, {**L, "x_in": A["hin"], "x_out": out})
        elif only == "mlp":
            mlp_phase(nc, c, A, 0, A["hin"], A["hin"], hid[1])
            mlp_phase(nc, c, A, 1, A["hin"], hid[1], out)
        elif only == "l1":
            single_head_phase(nc, c, A, A["hin"], out)
        else:
            attention_phase(nc, c, A, l0)
            mlp_phase(nc, c, A, 0, hid[0], hid[0], hid[1])
            mlp_phase(nc, c, A, 1, hid[0], hid[1], hid[2])
            single_head_phase(nc, c, A, hid[2], hid[3])
            attention_phase(nc, c, A, l2)
            attention_phase(nc, c, A, l3)


def kernel(**inputs):
    import numpy as _np
    import concourse.bacc as _bacc
    from concourse import mybir as _mybir
    from concourse.bass_utils import run_bass_kernel_spmd as _run

    flat = {"x": (NB * S, D), "ctx_2048": (NB * S, D), "mask_Bx1xSxS2_ff0": (NB * S, S), "L1_xattn_alpha": (1,)}
    nc = _bacc.Bacc("TRN2", target_bir_lowering=False, num_devices=1)
    arrays, aps = {}, {}
    for name, a in inputs.items():
        a = _np.ascontiguousarray(a)
        if name in flat:
            a = a.reshape(flat[name])
        if name == "mask_BxS2_bf1":
            a = a.view(_np.uint8)
        arrays[f"in_{name}"] = a
        aps[name] = nc.dram_tensor(f"in_{name}", a.shape, _mybir.dt.from_np(a.dtype), kind="ExternalInput").ap()
    out = nc.dram_tensor("out_x", (NB * S, D), F32, kind="ExternalOutput").ap()
    build(nc, aps, out)
    r = _run(nc, [arrays], core_ids=[0])
    return r.results[0]["out_x"].reshape(NB, S, D)
```

```python
from contextlib import ExitStack

import concourse.bass as bass
from concourse import mybir

F32 = mybir.dt.float32
F32R = mybir.dt.float32r
U8 = mybir.dt.uint8
ALU = mybir.AluOpType
ACT = mybir.ActivationFunctionType
AX_X = mybir.AxisListType.X

P = 128
D = 512
KC = D // P
NB = 8
S = 256
TT = S // P
INNER = 4 * D
BANK = 512
STEPS = 4
HI, LO = 0, 1
MASKED = -(2.0 ** 127)
PAIRS = ((HI, HI), (HI, LO), (LO, HI))


def wait(eng, sem, value):
    if isinstance(value, int) and value <= 0:
        return
    eng.wait_ge(sem, value)


def rows_of(x, b):
    return x[bass.ds(b * S, S)].rearrange("(t p) n -> p t n", p=P)


class Buffers:

    def __init__(self, nc, ctx, tag):
        self.nc, self.ctx, self.tag, self.sems = nc, ctx, tag, []
        ctx.callback(self.clear)

    def sb(self, name, shape, dt=F32):
        return self.ctx.enter_context(self.nc.sbuf_tensor(f"{self.tag}_{name}", shape, dt))

    def sem(self, name):
        self.sems.append(self.nc.alloc_semaphore(name=f"{self.tag}_{name}"))
        return self.sems[-1]

    def clear(self):
        self.nc.clear_and_free_semaphores(self.sems)
        self.nc.all_engine_barrier()


def setup_phase(nc, c, A):
    with ExitStack() as ctx:
        al = Buffers(nc, ctx, "set")
        stage = al.sb("vec_rows", [32, P])
        m8 = al.sb("m8", [NB, S], U8)
        m0, m1 = c["mask_rows"]
        any_key, guard = al.sb("any_key", [NB, 1]), al.sb("guard", [NB, 1])
        any_done = al.sem("any_done")
        loaded, zeroed, ident_done = al.sem("loaded"), al.sem("zeroed"), al.sem("ident_done")
        turned, cols_done, m0_done, m1_done = (al.sem(n) for n in ("turned", "cols_done", "m0_done", "m1_done"))
        block = ctx.enter_context(nc.Block())
        vecs = [("L0_xattn_q_b", 4), ("L0_xattn_k_b", 4), ("L2_xattn_bq", 4), ("L2_xattn_bk", 1), ("L0_xattn_fc_b", 16)]

        @block.sync
        def _(sp):
            row = 0
            for name, n in vecs:
                sp.dma_start(stage[row:row + n, :], A[name].rearrange("(r p) -> r p", p=P)).then_inc(loaded, 16)
                c["col"][name] = row
                row += n
            sp.dma_start(m8[:], A["mask_BxS2_bf1"]).then_inc(loaded, 16)
            sp.wait_ge(m0_done, 1)
            for sem, m, dram in ((m0_done, m0, c["mask_min"]), (m1_done, m1, c["mask_inf"])):
                sp.wait_ge(sem, 1)
                sp.dma_start(dram.rearrange("b (h t) -> b h t", h=4),
                             m[:].unsqueeze(1).broadcast_to([NB, 4, S])).then_inc(c["mask_stored"], 16)

        @block.gpsimd
        def _(pool):
            nc.gpsimd.memset(c["half"][:], -0.5)
            nc.gpsimd.memset(c["ident"][:], 0.0).then_inc(zeroed, 1)
            pool.wait_ge(zeroed, 1)
            nc.gpsimd.affine_select(out=c["ident"][:], in_=c["ident"][:], compare_op=ALU.not_equal, fill=1.0,
                                    base=0, pattern=[[-1, P]], channel_multiplier=1).then_inc(ident_done, 1)

        @block.tensor
        def _(pe):
            pe.wait_ge(loaded, 16 * (len(vecs) + 1))
            pe.wait_ge(ident_done, 1)
            nc.tensor.transpose(c["ps"][:, 0, 0:29], stage[0:29, :], c["ident"][0:29, 0:29]).then_inc(turned, 1)

        @block.vector
        def _(dve):
            dve.wait_ge(turned, 1)
            nc.vector.tensor_copy(c["cols"][:, 0:29], c["ps"][:, 0, 0:29]).then_inc(cols_done, 1)
            dve.wait_ge(cols_done, 1)
            nc.vector.tensor_scalar(c["cols"][:, 0:4], c["cols"][:, 0:4], 32.0 ** -0.5, None, ALU.mult)
            nc.vector.tensor_scalar(c["cols"][:, 8:12], c["cols"][:, 8:12], 0.25, None, ALU.mult)
            dve.wait_ge(loaded, 16 * (len(vecs) + 1))
            nc.vector.tensor_scalar(m0[:], m8[:], -1.0, -MASKED, ALU.add, ALU.mult).then_inc(m0_done, 1)
            dve.wait_ge(m0_done, 1)
            nc.vector.tensor_reduce(any_key[:], m8[:], AX_X, ALU.max).then_inc(any_done, 1)
            dve.wait_ge(any_done, 1)
            nc.vector.reciprocal(guard[:], any_key[:]).then_inc(any_done, 1)
            dve.wait_ge(any_done, 2)
            nc.vector.scalar_tensor_tensor(guard[:], any_key[:], guard[:, 0:1], any_key[:], ALU.mult, ALU.subtract).then_inc(any_done, 1)
            dve.wait_ge(any_done, 3)
            nc.vector.tensor_scalar(m1[:], m0[:], guard[:, 0:1], None, ALU.add).then_inc(m1_done, 1)


def attention_phase(nc, c, A, L):
    x_in, x_out, ctx_in = L["x_in"], L["x_out"], A["ctx_2048"]
    HS, HD, GQA = L["heads"] // STEPS, L["hd"], L["gqa"]
    NPAIR = HS // 2
    NK = L["nk"]
    BASE = 3 * HD
    KROWS = BASE if GQA else BASE + 1
    UNITS = 2 * NPAIR
    W_T = L["transposed"]
    post_ln, ln_x, ln_c = L["post_ln"], L["ln_x"], L["ln_c"]
    has_ln = ln_x or ln_c
    ps, ident = c["ps"], c["ident"]
    B_QK, B_OT, B_A, B_PT = 0, 3, 4, 6
    T_BANK = {("y", 0): 2, ("y", 1): 1, ("BT", 0): 2, ("O", 0): 1, ("BT", 1): 2, ("O", 1): 1, ("BT", 2): 2,
              ("V", 0): 1, ("x", 0): B_QK, ("x", 1): 2, ("V", 1): 1, ("BT", 3): B_QK, ("c", 0): 2, ("c", 1): 1}

    with ExitStack() as ctx:
        al = Buffers(nc, ctx, L["tag"])
        wq = al.sb("wq", [P, 2, KC, D], F32R)
        wk = al.sb("wk", [P, 2, KC, NK], F32R)
        wv = al.sb("wv", [P, 2, KC, NK], F32R)
        wo = al.sb("wo", [P, 2, KC, D], F32R)
        xin = al.sb("xin", [P, TT, D])
        cin = al.sb("cin", [P, TT, D])
        norm = al.sb("norm", [P, TT, D]) if has_ln else None
        xsrc = norm if ln_x else xin
        csrc = norm if ln_c else cin
        xT = al.sb("xT", [P, 2, KC, S], F32R)
        cT = al.sb("cT", [P, 2, KC, S], F32R)
        yT = al.sb("yT", [P, 2, KC, S], F32R)
        NE = 2 if GQA else 4
        E = al.sb("E", [P, 2, NE, S], F32R)
        EK = al.sb("EK", [P, 2, S], F32R) if GQA else None
        if GQA:
            qst = al.sb("qst", [64, STEPS, HS, S], F32R)
            kst = al.sb("kst", [64, STEPS, 2, S], F32R)
            V = al.sb("V", [P, TT, NK // HD, 32])
            mask_next, maskN = al.sb("mask_next", [P, TT, S]), al.sb("maskN", [P, TT, S])
        else:
            st = al.sb("st", [P, STEPS, HS, 2, S], F32R)
            V = al.sb("V", [P, TT, D])
        Pb = al.sb("Pb", [P, TT, HS, S])
        PTb = al.sb("PTb", [P, 2, TT, HS, S])
        OTs = al.sb("OTs", [P, BANK])
        y = al.sb("y", [P, TT, D])
        xres = al.sb("xres", [P, TT, D])
        xo = al.sb("xo", [P, TT, D])
        rows = {n: al.sb(f"row{i}", [P, w]) for i, (n, _, w) in enumerate(L["rows"])}
        negmax = al.sb("negmax", [P, TT, HS])
        nposmax = al.sb("nposmax", [P, TT, HS])
        sums = al.sb("sums", [P, STEPS, TT, HS])
        rcp2 = al.sb("rcp", [P, 2, 16])
        dummy = al.sb("dummy", [P, UNITS + 1])
        eps = al.sb("eps", [P, TT])
        stats = al.sb("stats", [P, TT, 6])
        mv = al.sb("mv", [P, TT, 2])
        veps = al.sb("veps", [P, TT])
        rstd = al.sb("rstd", [P, TT])
        pstats = al.sb("pstats", [P, TT, 6])
        pmv = al.sb("pmv", [P, TT, 2])
        pveps = al.sb("pveps", [P, TT])
        prstd = al.sb("prstd", [P, TT])
        gate = al.sb("gate", [P, 2])

        sem = {}
        for n in ("w_in0 w_in1 w_in2 row_in norm_in gate_in gate_done wT_mm w_hi w_lo x_in c_in xres_in mask_in out_st ek_w "
                  "pe_T act_hi dve_T pe_qk act_e dve_e pe_a dve_max act_exp pe_pt act_pt dve_pt pe_pv act_ot "
                  "dve_bs dve_mv pool_ve pool_rs dve_xn pool_g pool_b pool_res dve_rc dve_pbs dve_pmv "
                  "eps_set pool_pve pool_prs dve_pxn pool_pg pool_out ones_done dve_mask").split():
            sem[n] = al.sem(n)
        e_written = [al.sem(f"e_written{i}") for i in range(2)]
        stacked = [al.sem(f"stacked{g}") for g in range(STEPS)]
        block = ctx.enter_context(nc.Block())

        lead = ["c", 0, 1, "x"] if ln_x else ["x", 0, 1, "c"] if ln_c else ["x", "c", 0, 1]
        early = [r for r in L["rows"] if has_ln and r[0] in ("g", "b")]
        late = [r for r in L["rows"] if r not in early]

        LOOP = 2
        front, back, outp, nxt = (lambda v: v < NB), (lambda v: 1 <= v <= NB), (lambda v: v >= 2), (lambda v: v < NB - 1)

        def items(v):
            if v < 0:
                return [(k, t) for k in lead if k in ("x", "c") for t in range(TT)]
            has = {"y": outp(v), "O": outp(v), "BT": back(v), "V": front(v), "x": nxt(v), "c": nxt(v)}
            out = [k for k in T_BANK if has[k[0]]]
            return out

        def count(v, of=len):
            return sum(of(items(w)) for w in range(-1, v))

        def turned(seq):
            return sum(k in "xyc" for k, _ in seq)

        def ahead(v, u, of=len):
            return u * of(items(LOOP)) + count(LOOP, of) if v == LOOP else count(v, of)

        def item_no(v, u, key):
            return ahead(v, u) + items(v).index(key)

        def turn_no(v, u, key):
            return ahead(v, u, turned) + turned(items(v)[:items(v).index(key)])

        def before_in_bank(v, u, key):
            seq = items(v)
            i = seq.index(key)
            same = [j for j in range(i) if T_BANK[seq[j]] == T_BANK[key]]
            if same:
                return ahead(v, u) + same[-1] + 1
            prev = items(v - 1)
            same = [j for j, k in enumerate(prev) if T_BANK[k] == T_BANK[key]]
            return ahead(v, u) - (len(prev) - 1 - same[-1]) if same else ahead(v, u)

        def bodies(eng, body):
            body(0, 0, None, None, 0)
            body(1, 1, 0, None, 0)
            with eng.Fori(0, NB - 1 - LOOP) as u:
                body(LOOP, u + 2, u + 1, u, u)
            body(NB - 1, NB - 1, NB - 2, NB - 3, 0)
            body(NB, None, NB - 1, NB - 2, 0)
            body(NB + 1, None, None, NB - 1, 0)

        def back_step(vf, vb, g, lag):
            b, gg = (vf, g - lag) if g >= lag else (vb, g - lag + STEPS)
            return None if b is None else (b, gg)

        def unit(b, g, i):
            return b * (STEPS * UNITS) + (g * UNITS + i)

        wunits = [("q", A[L["wq"]], wq, D, L["qscale"]), ("k", A[L["wk"]], wk, NK, 1.0),
                  ("v", A[L["wv"]], wv, NK, 1.0), ("o", A[L["wo"]], wo, D, L["oscale"])]
        flat = PTb[:].rearrange("p i a b c -> p (i a b c)")
        stages = [Pb[:].rearrange("p a b c -> p (a b c)")[:, 0:KC * D], flat[:, 0:KC * D], flat[:, KC * D:2 * KC * D]]

        def stage_of(j, n):
            return stages[j % 3][:, 0:KC * n].rearrange("p (k n) -> p k n", k=KC)

        n_reads = 6 if GQA else 5

        @block.sync
        def _(sp):
            first = {"x": lambda: sp.dma_start(xin[:], rows_of(x_in, 0)).then_inc(sem["x_in"], 16),
                     "c": lambda: sp.dma_start(cin[:], rows_of(ctx_in, 0)).then_inc(sem["c_in"], 16)}
            for k in ("x", "c") if ln_x else ("c", "x"):
                first[k]()
            for j, (_, src, _, n, _) in enumerate(wunits):
                if j == 1:
                    for r, rsrc, w in early:
                        sp.dma_start(rows[r][:], A[rsrc].partition_broadcast(P)).then_inc(sem["norm_in"], 16)
                if j == 3:
                    for r, rsrc, w in late:
                        sp.dma_start(rows[r][:], A[rsrc].partition_broadcast(P)).then_inc(sem["row_in"], 16)
                    if L["oscale"] is None:
                        sp.dma_start(gate[:, 0:1], A["L3_xattn_gate"].partition_broadcast(P)).then_inc(sem["gate_in"], 16)
                    sp.wait_ge(sem["w_lo"], KC)
                sp.dma_start(stage_of(j, n), src.rearrange("(k p) n -> p k n", p=P)).then_inc(sem[f"w_in{j % 3}"], 16)

            def body(v, vf, vb, vo, u):
                F, B, O, N = front(v), back(v), outp(v), nxt(v)
                if N:
                    sp.wait_ge(sem["pe_T"], ahead(v, u))
                    if has_ln:
                        wait(sp, sem["dve_xn"], vf * TT + TT)
                    sp.dma_start(xin[:], rows_of(x_in, vf + 1)).then_inc(sem["x_in"], 16)
                    sp.dma_start(cin[:], rows_of(ctx_in, vf + 1)).then_inc(sem["c_in"], 16)
                if GQA and F:
                    wait(sp, sem["dve_mask"], vf)
                    sp.dma_start(mask_next[:], A["mask_Bx1xSxS2_ff0"][bass.ds(vf * S, S)].rearrange(
                        "(t p) k -> p t k", p=P)).then_inc(sem["mask_in"], 16)
                for g in range(STEPS):
                    if not F:
                        continue
                    par = g % 2
                    sp.wait_ge(sem["act_e"], (vf * STEPS + g) + 1)
                    sp.wait_ge(sem["dve_e"], (vf * STEPS + g) + 1)
                    scr = c["scr"][g]
                    sp.dma_start(scr[:, 0:NE, :], E[:, par].bitcast(F32)).then_inc(e_written[par], 16)
                    if GQA and g == 0:
                        filled = vf * (16 * n_reads)
                        for gg in range(STEPS):
                            wait(sp, stacked[gg], filled)
                        sp.dma_start(c["scrk"], EK[:].bitcast(F32)).then_inc(sem["ek_w"], 16)
                        sp.wait_ge(sem["ek_w"], vf * 16 + 16)
                    written = (vf * 2 + g // 2) * 16 + 16
                    if B:
                        sp.wait_ge(sem["pe_a"], unit(vb, g, UNITS))
                    sp.wait_ge(e_written[par], written)
                    if not GQA and v == 0 and g == 0:
                        sp.wait_ge(c["mask_stored"], 32)
                    if GQA:
                        q = [scr[:, j, :].rearrange("(h d) t -> d h t", d=HD) for j in range(2)]
                        k = [c["scrk"][2 * HD * g:2 * HD * (g + 1), j, :].rearrange("(h d) t -> d h t", d=HD) for j in range(2)]
                        for r, (jq, jk) in enumerate(PAIRS):
                            pr = slice(r * HD, (r + 1) * HD)
                            sp.dma_start(qst[pr, g].bitcast(F32), q[jq]).then_inc(stacked[g], 16)
                            sp.dma_start(kst[pr, g].bitcast(F32), k[jk]).then_inc(stacked[g], 16)
                    else:
                        split = scr.rearrange("(h d) j t -> d h j t", d=HD)
                        sp.dma_start(st[0:HD, g, :, 0, :].bitcast(F32), split[:, :, 0, :]).then_inc(stacked[g], 16)
                        sp.dma_start(st[0:HD, g, :, 1, :].bitcast(F32), split[:, :, 3, :]).then_inc(stacked[g], 16)
                        sp.dma_start(st[HD:2 * HD, g].bitcast(F32), split[:, :, 0:2, :]).then_inc(stacked[g], 16)
                        sp.dma_start(st[2 * HD:3 * HD, g].bitcast(F32), split[:, :, 2:4, :]).then_inc(stacked[g], 16)
                        sp.dma_start(st[3 * HD:3 * HD + 1, g, :, 1, :].bitcast(F32),
                                     L["mask"][bass.ds(vf, 1)].rearrange("b (h t) -> b h t", h=HS)).then_inc(stacked[g], 16)
                if B:
                    sp.wait_ge(sem["dve_T"], item_no(v, u, ("O", 1) if O else ("BT", 0)) + 1)
                    sp.dma_start(xres[:], rows_of(x_in, vb)).then_inc(sem["xres_in"], 16)
                if O:
                    if post_ln:
                        sp.wait_ge(sem["pool_out"], vo * TT + TT)
                    else:
                        sp.wait_ge(sem["dve_T"], item_no(v, u, ("O", 1)) + 1)
                    sp.dma_start(rows_of(x_out, vo), xo[:]).then_inc(sem["out_st"], 16)

            bodies(sp, body)
            sp.wait_ge(sem["out_st"], 16 * NB)

        @block.gpsimd
        def _(pool):
            nc.gpsimd.memset(eps[:], L["eps"]).then_inc(sem["eps_set"], 1)
            pool.wait_ge(sem["eps_set"], 1)
            if GQA:
                nc.gpsimd.memset(V[:], 1.0).then_inc(sem["ones_done"], 1)
            else:
                nc.gpsimd.memset(st[3 * HD:3 * HD + 1, :, :, 0, :].bitcast(F32), 1.0).then_inc(sem["ones_done"], 1)
            pool.wait_ge(sem["ones_done"], 1)

            def norm_rows(n):
                pool.wait_ge(sem["dve_mv"], n * TT + TT)
                nc.gpsimd.tensor_tensor(veps[:], mv[:, :, 1], eps[:], ALU.add).then_inc(sem["pool_ve"], 1)
                pool.wait_ge(sem["pool_ve"], n + 1)
                nc.gpsimd.tensor_tensor(rstd[:], veps[:], c["half"][:, 0:TT], ALU.pow).then_inc(sem["pool_rs"], 1)
                if isinstance(n, int) and n == 0:
                    pool.wait_ge(sem["norm_in"], 16 * len(early))
                for t in range(TT):
                    pool.wait_ge(sem["dve_xn"], n * TT + (t + 1))
                    nc.gpsimd.tensor_tensor(norm[:, t], norm[:, t], rows["g"][:], ALU.mult).then_inc(sem["pool_g"], 1)
                    pool.wait_ge(sem["pool_g"], n * TT + (t + 1))
                    nc.gpsimd.tensor_tensor(norm[:, t], norm[:, t], rows["b"][:], ALU.add).then_inc(sem["pool_b"], 1)

            if has_ln:
                norm_rows(0)
            if late:
                pool.wait_ge(sem["row_in"], 16 * len(late))

            def body(v, vf, vb, vo, u):
                if outp(v):
                    pool.wait_ge(sem["xres_in"], vo * 16 + 16)
                    for t in range(TT):
                        if "ob" in rows:
                            nc.gpsimd.tensor_tensor(xres[:, t], xres[:, t], rows["ob"][:], ALU.add).then_inc(sem["pool_res"], 1)
                if has_ln and nxt(v):
                    norm_rows(vf + 1)
                if outp(v) and post_ln:
                    pool.wait_ge(sem["dve_pmv"], vo * TT + TT)
                    nc.gpsimd.tensor_tensor(pveps[:], pmv[:, :, 1], eps[:], ALU.add).then_inc(sem["pool_pve"], 1)
                    pool.wait_ge(sem["pool_pve"], vo + 1)
                    nc.gpsimd.tensor_tensor(prstd[:], pveps[:], c["half"][:, 0:TT], ALU.pow).then_inc(sem["pool_prs"], 1)
                    for t in range(TT):
                        pool.wait_ge(sem["dve_pxn"], vo * TT + (t + 1))
                        nc.gpsimd.tensor_tensor(xo[:, t], xo[:, t], rows["g"][:], ALU.mult).then_inc(sem["pool_pg"], 1)
                        pool.wait_ge(sem["pool_pg"], vo * TT + (t + 1))
                        nc.gpsimd.tensor_tensor(xo[:, t], xo[:, t], rows["b"][:], ALU.add).then_inc(sem["pool_out"], 1)

            bodies(pool, body)

        @block.scalar
        def _(act):
            def high_weights(j):
                _, _, w, n, scale = wunits[j]
                if scale is None:
                    act.wait_ge(sem["gate_in"], 16)
                    nc.scalar.activation(gate[:, 1:2], gate[:, 0:1], ACT.Tanh).then_inc(sem["gate_done"], 1)
                    act.wait_ge(sem["gate_done"], 1)
                if not W_T:
                    act.wait_ge(sem[f"w_in{j % 3}"], 16 * (j // 3 + 1))
                for k in range(KC):
                    if W_T:
                        act.wait_ge(sem["wT_mm"], j * KC + (k + 1))
                    src = ps[:, 4 + k, :] if W_T else stage_of(j, n)[:, k]
                    if scale is None:
                        nc.scalar.activation(w[:, HI, k], src, ACT.Identity, scale=gate[:, 1:2]).then_inc(sem["w_hi"], 1)
                    else:
                        nc.scalar.activation(w[:, HI, k], src, ACT.Copy, scale=scale).then_inc(sem["w_hi"], 1)

            def high(v, u, kind, dst):
                for t in range(TT):
                    act.wait_ge(sem["pe_T"], item_no(v, u, (kind, t)) + 1)
                    nc.scalar.activation(dst[:, HI, :, t * P:(t + 1) * P],
                                         ps[:, T_BANK[kind, t], :].rearrange("p (k s) -> p k s", k=KC),
                                         ACT.Copy).then_inc(sem["act_hi"], 1)

            for k in lead:
                if k in ("x", "c"):
                    high(-1, 0, k, xT if k == "x" else cT)
                else:
                    high_weights(k)

            def body(v, vf, vb, vo, u):
                F, B, O, N = front(v), back(v), outp(v), nxt(v)
                for g in range(STEPS):
                    sa = back_step(vf, vb, g, 2)
                    sp_ = back_step(vf, vb, g, 3)
                    for p in range(NPAIR):
                        if F and p == NPAIR - 1:
                            high_qk(vf, g)
                        if B and p == NPAIR - 1:
                            act.wait_ge(sem["pe_pv"], (vb * STEPS + g) + 1)
                            if g:
                                act.wait_ge(sem["pe_T"], item_no(v, u, ("BT", g - 1)) + 1)
                            nc.scalar.activation(OTs[:, 0:L["ot"]], ps[:, B_OT, 0:L["ot"]], ACT.Copy).then_inc(sem["act_ot"], 1)
                        if sp_ is not None:
                            n = unit(sp_[0], sp_[1], 2 * p)
                            act.wait_ge(sem["pe_pt"], n + 1)
                            nc.scalar.activation(PTb[:, sp_[1] % 2, 0, 2 * p:2 * p + 2, :],
                                                 ps[:, B_PT, :].rearrange("p (h s) -> p h s", h=2),
                                                 ACT.Copy).then_inc(sem["act_pt"], 1)
                        if O and g == 0 and p == 0:
                            high(v, u, "y", yT)
                        if sa is not None:
                            for t in range(TT):
                                n = unit(sa[0], sa[1], 2 * p + t)
                                act.wait_ge(sem["dve_max"], n + 1)
                                for h in (2 * p, 2 * p + 1):
                                    if GQA:
                                        last = nc.scalar.activation(Pb[:, t, h], Pb[:, t, h], ACT.Exp, bias=negmax[:, t, h:h + 1],
                                                                    scale=-1.0)
                                    else:
                                        last = nc.scalar.activation(
                                            Pb[:, t, h], ps[:, B_A + t, (h % 2) * S:(h % 2 + 1) * S], ACT.Exp,
                                            bias=negmax[:, t, h:h + 1], accum_out=sums[:, sa[1], t, h:h + 1])
                                last.then_inc(sem["act_exp"], 1)
                    if v == 0 and g < 2:
                        high_weights(2 + g)
                if N:
                    high(v, u, "x", xT)
                    high(v, u, "c", cT)

            def high_qk(vf, g):
                act.wait_ge(sem["pe_qk"], (vf * STEPS + g) + 1)
                wait(act, e_written[g % 2], (vf * 2 + g // 2) * 16)
                kcol = None if L["kcol"] is None else L["kcol"] + (0 if GQA else g)
                kbias = None if kcol is None else c["cols"][:, kcol:kcol + 1]
                qbias = None if L["qcol"] is None else c["cols"][:, L["qcol"] + g:L["qcol"] + g + 1]
                if GQA:
                    if g == 0:
                        wait(act, sem["ek_w"], vf * 16)
                        nc.scalar.activation(EK[:, 0], ps[:, B_QK, S:2 * S], ACT.Identity, bias=kbias)
                    nc.scalar.activation(E[:, g % 2, 0], ps[:, B_QK, 0:S], ACT.Identity, bias=qbias).then_inc(sem["act_e"], 1)
                elif qbias is None:
                    nc.scalar.activation(E[:, g % 2, 0:4:3, :], ps[:, B_QK, :].rearrange("p (j s) -> p j s", j=2),
                                         ACT.Copy).then_inc(sem["act_e"], 1)
                else:
                    nc.scalar.activation(E[:, g % 2, 0], ps[:, B_QK, 0:S], ACT.Identity, bias=qbias)
                    nc.scalar.activation(E[:, g % 2, 3], ps[:, B_QK, S:2 * S], ACT.Identity, bias=kbias).then_inc(sem["act_e"], 1)

            bodies(act, body)

        @block.vector
        def _(dve):
            def stats_of(src, sm, n, tiles_stats, tiles_mv, bs, mvs, ready):
                for t in range(TT):
                    ready(t)
                    nc.vector.bn_stats(tiles_stats[:, t], src[:, t]).then_inc(sem[bs], 1)
                dve.wait_ge(sem[bs], n * TT + TT)
                nc.vector.memset(dummy[:, UNITS:UNITS + 1], 0.0)
                for t in range(TT):
                    nc.vector.bn_aggr(tiles_mv[:, t], tiles_stats[:, t]).then_inc(sem[mvs], 1)

            lsrc = xin if ln_x else cin

            def norm_stats(n):
                stats_of(lsrc, None, n, stats, mv, "dve_bs", "dve_mv",
                         lambda t: dve.wait_ge(sem["x_in" if ln_x else "c_in"], n * 16 + 16) if t == 0 else None)

            def norm_apply(n):
                dve.wait_ge(sem["pool_rs"], n + 1)
                for t in range(TT):
                    nc.vector.tensor_scalar(norm[:, t], lsrc[:, t], mv[:, t, 0:1], rstd[:, t:t + 1],
                                            ALU.subtract, ALU.mult).then_inc(sem["dve_xn"], 1)

            if has_ln:
                norm_stats(0)
                norm_apply(0)

            def low_weights(j):
                _, _, w, n, scale = wunits[j]
                for k in range(KC):
                    dve.wait_ge(sem["w_hi"], j * KC + (k + 1))
                    src = ps[:, 4 + k, :] if W_T else stage_of(j, n)[:, k]
                    nc.vector.scalar_tensor_tensor(w[:, LO, k], src, gate[:, 1:2] if scale is None else scale,
                                                   w[:, HI, k], ALU.mult, ALU.subtract).then_inc(sem["w_lo"], 1)

            def low(v, u, kind, dst):
                for t in range(TT):
                    dve.wait_ge(sem["act_hi"], turn_no(v, u, (kind, t)) + 1)
                    nc.vector.tensor_tensor(dst[:, LO, :, t * P:(t + 1) * P],
                                            ps[:, T_BANK[kind, t], :].rearrange("p (k s) -> p k s", k=KC),
                                            dst[:, HI, :, t * P:(t + 1) * P], ALU.subtract).then_inc(sem["dve_T"], 1)

            for k in lead:
                if k in ("x", "c"):
                    low(-1, 0, k, xT if k == "x" else cT)
                else:
                    low_weights(k)
            if late:
                dve.wait_ge(sem["row_in"], 16 * len(late))
            dve.wait_ge(sem["ones_done"], 1)

            def body(v, vf, vb, vo, u):
                F, B, O, N = front(v), back(v), outp(v), nxt(v)
                for g in range(STEPS):
                    if has_ln and N and g == 1:
                        norm_stats(vf + 1)
                    if has_ln and N and g == 2:
                        dve.wait_ge(sem["pe_T"], ahead(v, u))
                        norm_apply(vf + 1)
                    sa = back_step(vf, vb, g, 2)
                    sp_ = back_step(vf, vb, g, 3)
                    for p in range(NPAIR):
                        if sp_ is not None:
                            n = unit(sp_[0], sp_[1], 2 * p + 1)
                            dve.wait_ge(sem["pe_pt"], n + 1)
                            nc.vector.tensor_copy(PTb[:, sp_[1] % 2, 1, 2 * p:2 * p + 2, :],
                                                  ps[:, B_PT + 1, :].rearrange("p (h s) -> p h s", h=2)).then_inc(sem["dve_pt"], 1)
                        if F and p == NPAIR - 1:
                            low_qk(vf, g)
                        if O and g == 0 and p == 0:
                            low(v, u, "y", yT)
                        if sa is not None:
                            for t in range(TT):
                                n = unit(sa[0], sa[1], 2 * p + t)
                                if GQA and sa[1] == 0 and p == 0 and t == 0:
                                    dve.wait_ge(sem["mask_in"], sa[0] * 16 + 16)
                                    nc.vector.tensor_copy(maskN[:], mask_next[:]).then_inc(sem["dve_mask"], 1)
                                    dve.wait_ge(sem["dve_mask"], sa[0] + 1)
                                dve.wait_ge(sem["pe_a"], n + 1)
                                if GQA:
                                    nc.vector.memset(dummy[:, 2 * p + t:2 * p + t + 1], 0.0)
                                    for h in (2 * p, 2 * p + 1):
                                        last = nc.vector.tensor_tensor_reduce(
                                            Pb[:, t, h], ps[:, B_A + t, (h % 2) * S:(h % 2 + 1) * S], maskN[:, t, :],
                                            -1.0, 3.0e38, ALU.add, ALU.min, negmax[:, t, h:h + 1])
                                    last.then_inc(sem["dve_max"], 1)
                                else:
                                    nc.vector.tensor_reduce(negmax[:, t, 2 * p:2 * p + 2],
                                                            ps[:, B_A + t, :].rearrange("p (h s) -> p h s", h=2),
                                                            AX_X, ALU.max, negate=True).then_inc(sem["dve_max"], 1)
                    if O and g in (1, 2):
                        add_output(v, u, vo, g - 1)
                    if F and g == 3:
                        values(v, u, 0)
                    if B and g < 3:
                        divide(v, u, vb, g)
                    if v == 0 and g < 2:
                        low_weights(2 + g)
                if O and post_ln:
                    stats_of(xo, None, vo, pstats, pmv, "dve_pbs", "dve_pmv",
                             lambda t: dve.wait_ge(sem["dve_T"], item_no(v, u, ("O", 1)) + 1) if t == 0 else None)
                if N:
                    low(v, u, "x", xT)
                if F:
                    values(v, u, 1)
                if B:
                    divide(v, u, vb, 3)
                if N:
                    low(v, u, "c", cT)
                if O and post_ln:
                    dve.wait_ge(sem["pool_prs"], vo + 1)
                    for t in range(TT):
                        nc.vector.tensor_scalar(xo[:, t], xo[:, t], pmv[:, t, 0:1], prstd[:, t:t + 1],
                                                ALU.subtract, ALU.mult).then_inc(sem["dve_pxn"], 1)

            def values(v, u, t):
                dve.wait_ge(sem["pe_T"], item_no(v, u, ("V", t)) + 1)
                bank = ps[:, T_BANK["V", t], :]
                if GQA:
                    nc.vector.tensor_tensor(V[:, t, :, 0:HD], bank[:, 0:NK].rearrange("p (h d) -> p h d", d=HD),
                                            rows["vb"][:].rearrange("p (h d) -> p h d", d=HD), ALU.add).then_inc(sem["dve_T"], 1)
                elif "vb" in rows:
                    nc.vector.tensor_tensor(V[:, t], bank, rows["vb"][:], ALU.add).then_inc(sem["dve_T"], 1)
                else:
                    nc.vector.tensor_copy(V[:, t], bank).then_inc(sem["dve_T"], 1)

            def low_qk(vf, g):
                dve.wait_ge(sem["act_e"], (vf * STEPS + g) + 1)
                if GQA:
                    kb = c["cols"][:, L["kcol"]:L["kcol"] + 1]
                    qb = c["cols"][:, L["qcol"] + g:L["qcol"] + g + 1]
                    if g == 0:
                        nc.vector.scalar_tensor_tensor(EK[:, 1], ps[:, B_QK, S:2 * S], kb, EK[:, 0], ALU.add, ALU.subtract)
                    nc.vector.scalar_tensor_tensor(E[:, g % 2, 1], ps[:, B_QK, 0:S], qb, E[:, g % 2, 0],
                                                   ALU.add, ALU.subtract).then_inc(sem["dve_e"], 1)
                else:
                    for j, (lo_, hi_, col) in enumerate(((2, 0, L["qcol"]), (1, 3, L["kcol"]))):
                        last = nc.vector.scalar_tensor_tensor(
                            E[:, g % 2, lo_], ps[:, B_QK, j * S:(j + 1) * S],
                            0.0 if col is None else c["cols"][:, col + g:col + g + 1], E[:, g % 2, hi_], ALU.add, ALU.subtract)
                    last.then_inc(sem["dve_e"], 1)

            def divide(v, u, vb, g):
                dve.wait_ge(sem["pe_T"], item_no(v, u, ("BT", g)) + 1)
                bank = ps[:, T_BANK["BT", g], :]
                rcp = rcp2[:, g % 2]
                if GQA:
                    o = bank.rearrange("p (u t h d) -> p u t h d", u=2, t=TT, h=4)
                    rc = rcp.rearrange("p (u t h) -> p u t h", u=2, t=TT)
                    nc.vector.reciprocal(rcp.rearrange("p (a h) -> p a h", a=4),
                                         bank.rearrange("p (a h d) -> p a h d", a=4, h=4)[:, :, :, HD]).then_inc(sem["dve_rc"], 1)
                    dve.wait_ge(sem["dve_rc"], (vb * STEPS + g) + 1)
                    for w in range(2):
                        yv = y[:, :, g * P + w * 64:g * P + (w + 1) * 64].rearrange("p t (h d) -> p t h d", h=4)
                        last = nc.vector.tensor_tensor(yv, o[:, w, :, :, 0:HD],
                                                       rc[:, w].unsqueeze(3).broadcast_to([P, TT, 4, HD]), ALU.mult)
                    last.then_inc(sem["dve_T"], 1)
                else:
                    nc.vector.reciprocal(rcp[:, 0:TT * HS], sums[:, g].rearrange("p t h -> p (t h)")).then_inc(sem["dve_rc"], 1)
                    dve.wait_ge(sem["dve_rc"], (vb * STEPS + g) + 1)
                    nc.vector.tensor_tensor(
                        y[:, :, g * P:(g + 1) * P].rearrange("p t (h d) -> p t h d", h=HS),
                        bank[:, 0:TT * P].rearrange("p (t h d) -> p t h d", t=TT, h=HS),
                        rcp[:, 0:TT * HS].rearrange("p (t h) -> p t h", t=TT).unsqueeze(3).broadcast_to([P, TT, HS, HD]),
                        ALU.mult).then_inc(sem["dve_T"], 1)

            def add_output(v, u, vo, t):
                if t == 0:
                    wait(dve, sem["out_st"], vo * 16)
                    if "ob" in rows:
                        dve.wait_ge(sem["pool_res"], vo * TT + TT)
                    else:
                        dve.wait_ge(sem["xres_in"], vo * 16 + 16)
                dve.wait_ge(sem["pe_T"], item_no(v, u, ("O", t)) + 1)
                nc.vector.tensor_tensor(xo[:, t], ps[:, T_BANK["O", t], :], xres[:, t],
                                        ALU.add).then_inc(sem["dve_T"], 1)

            bodies(dve, body)

        @block.tensor
        def _(pe):
            def turn_weights(j):
                pe.wait_ge(sem[f"w_in{j % 3}"], 16 * (j // 3 + 1))
                src = stage_of(j, D)
                for k in range(KC):
                    if j:
                        pe.wait_ge(sem["w_lo"], (j - 1) * KC + (k + 1))
                    for o in range(KC):
                        last = nc.tensor.transpose(ps[:, 4 + k, o * P:(o + 1) * P], src[:, o, k * P:(k + 1) * P], ident[:])
                    last.then_inc(sem["wT_mm"], 1)

            def bank_free(v, u, key):
                wait(pe, sem["dve_T"], before_in_bank(v, u, key))

            def turn(v, u, kind, src, n=None):
                for t in range(TT):
                    if n is not None:
                        ready(kind, n, t)
                    bank_free(v, u, (kind, t))
                    for k in range(KC):
                        last = nc.tensor.transpose(ps[:, T_BANK[kind, t], k * P:(k + 1) * P], src[:, t, k * P:(k + 1) * P], ident[:])
                    last.then_inc(sem["pe_T"], 1)

            NM = len(PAIRS) * KC

            def token_product(kind, t, aT, w, width, part=range(NM)):
                for m in part:
                    (a, b), k = PAIRS[m // KC], m % KC
                    last = nc.tensor.matmul(ps[:, T_BANK[kind, t], 0:width], aT[:, a, k, t * P:(t + 1) * P], w[:, b, k, :],
                                            start=(m == 0), stop=(m == NM - 1))
                if part[-1] == NM - 1:
                    last.then_inc(sem["pe_T"], 1)

            def ready(name, n, t):
                if (ln_x if name == "x" else ln_c):
                    pe.wait_ge(sem["pool_b"], n * TT + (t + 1))
                elif t == 0:
                    pe.wait_ge(sem["x_in" if name == "x" else "c_in"], n * 16 + 16)

            for k in lead:
                if k == "x":
                    turn(-1, 0, "x", xsrc, 0)
                elif k == "c":
                    turn(-1, 0, "c", csrc, 0)
                elif W_T:
                    turn_weights(k)
            pe.wait_ge(sem["w_lo"], 2 * KC)
            pe.wait_ge(sem["ones_done"], 1)

            def qk_product(g, part, of):
                operands = [(0, wq, xT, g * P)]
                if not GQA or g == 0:
                    operands.append((S, wk, cT, 0 if GQA else g * P))
                n = NM * len(operands)
                for m in range(part * n // of, (part + 1) * n // of):
                    (col0, w, aT, n0), i = operands[m // NM], m % NM
                    (a, h), k = PAIRS[i // KC], i % KC
                    last = nc.tensor.matmul(ps[:, B_QK, col0:col0 + S], w[:, a, k, n0:n0 + P], aT[:, h, k, :],
                                            start=(i == 0), stop=(i == NM - 1))
                if part == of - 1:
                    last.then_inc(sem["pe_qk"], 1)

            def head_outputs(v, u, vb, g, p):
                if p == 0:
                    if g == 0:
                        pe.wait_ge(sem["dve_T"], ahead(v, u) - 2 if nxt(v - 1) else ahead(v, u))
                    pe.wait_ge(sem["act_pt"], (vb * STEPS + g) * NPAIR + NPAIR)
                    pe.wait_ge(sem["dve_pt"], (vb * STEPS + g) * NPAIR + NPAIR)
                    wait(pe, sem["act_ot"], vb * STEPS + g)
                w, kt = p // TT, p % TT
                for j in range(4):
                    if GQA:
                        lhsT = V[:, kt, 2 * g + w, :]
                    else:
                        lhsT = V[:, kt, (4 * g + j) * HD:(4 * g + j + 1) * HD]
                    last = nc.tensor.matmul(ps[32 * j:32 * j + 32, B_OT, w * S:(w + 1) * S], lhsT,
                                            PTb[:, g % 2, kt, 4 * w + j, :], start=(kt == 0), stop=(kt == TT - 1))
                if p == NPAIR - 1:
                    last.then_inc(sem["pe_pv"], 1)

            def body(v, vf, vb, vo, u):
                F, B, O, N = front(v), back(v), outp(v), nxt(v)
                for g in range(STEPS):
                    if F:
                        if g == 0:
                            pe.wait_ge(sem["dve_T"], ahead(v, u) - (2 if v else 0))
                        wait(pe, sem["dve_e"], vf * STEPS + g)

                    sa = back_step(vf, vb, g, 2)
                    sp_ = back_step(vf, vb, g, 3)
                    for p in range(NPAIR):
                        if F:
                            qk_product(g, 2 * p, 2 * NPAIR - 1)
                        if B:
                            head_outputs(v, u, vb, g, p)
                        if sp_ is not None:
                            b, gg = sp_
                            for kt in range(TT):
                                pe.wait_ge(sem["act_exp"], unit(b, gg, 2 * p + 2))
                                wait(pe, sem["act_pt" if kt == 0 else "dve_pt"], (b * STEPS + gg) * NPAIR + p)
                                for hh in range(2):
                                    for t in range(TT):
                                        last = nc.tensor.transpose(ps[:, B_PT + kt, hh * S + t * P:hh * S + (t + 1) * P],
                                                                   Pb[:, t, 2 * p + hh, kt * P:(kt + 1) * P], ident[:])
                                last.then_inc(sem["pe_pt"], 1)
                        if O and g == 0 and p == 0:
                            pe.wait_ge(sem["dve_T"], ahead(v, u) - (2 if nxt(v - 1) else 0))
                            turn(v, u, "y", y)
                        if F and p < NPAIR - 1:
                            if g == 0 and p == 0:
                                pe.wait_ge(sem["dve_T"], ahead(v, u))
                            qk_product(g, 2 * p + 1, 2 * NPAIR - 1)
                        if sa is not None:
                            b, gg = sa
                            if v == 0 and g == 2 and p == 0:
                                pe.wait_ge(sem["w_lo"], 4 * KC)
                            if p == 0:
                                pe.wait_ge(stacked[gg], b * (16 * n_reads) + 16 * n_reads)
                            for t in range(TT):
                                wait(pe, sem["dve_max" if GQA else "act_exp"], unit(b, gg, 2 * p + t - 1))
                                for hh in range(2):
                                    h = 2 * p + hh
                                    if GQA:
                                        lhsT, rhs = qst[0:KROWS, gg, h, t * P:(t + 1) * P], kst[0:KROWS, gg, h // 4, :]
                                    else:
                                        lhsT, rhs = st[0:KROWS, gg, h, 0, t * P:(t + 1) * P], st[0:KROWS, gg, h, 1, :]
                                    last = nc.tensor.matmul(ps[:, B_A + t, hh * S:(hh + 1) * S], lhsT, rhs, start=True, stop=True)
                                last.then_inc(sem["pe_a"], 1)
                        part = range(p * NM // NPAIR, (p + 1) * NM // NPAIR)
                        if O and g in (1, 2):
                            if p == 0:
                                pe.wait_ge(sem["dve_T"], item_no(v, u, ("y", g - 1)) + 1)
                                bank_free(v, u, ("O", g - 1))
                            token_product("O", g - 1, yT, wo, D, part)
                        if F and g == 3:
                            if p == 0:
                                bank_free(v, u, ("V", 0))
                                if v == 0:
                                    pe.wait_ge(sem["w_lo"], 3 * KC)
                            token_product("V", 0, cT, wv, NK, part)
                    if B and g < 3:
                        turn_outputs(v, u, vb, g)
                    if v == 0 and g < 2 and W_T:
                        turn_weights(2 + g)
                if F:
                    pe.wait_ge(sem["dve_e"], vf * STEPS + STEPS)
                if N:
                    turn(v, u, "x", xsrc, vf + 1)
                if F:
                    bank_free(v, u, ("V", 1))
                    token_product("V", 1, cT, wv, NK)
                if B:
                    turn_outputs(v, u, vb, 3)
                if N:
                    turn(v, u, "c", csrc, vf + 1)

            def turn_outputs(v, u, vb, g):
                bank_free(v, u, ("BT", g))
                pe.wait_ge(sem["act_ot"], (vb * STEPS + g) + 1)
                for a in range(L["ot"] // P):
                    last = nc.tensor.transpose(ps[:, T_BANK["BT", g], a * P:(a + 1) * P], OTs[:, a * P:(a + 1) * P], ident[:])
                last.then_inc(sem["pe_T"], 1)

            bodies(pe, body)


def mlp_phase(nc, c, A, x_in, x_out):
    NJ = INNER // P
    NQ = NJ // 2
    RING = 4
    ps, ident = c["ps"], c["ident"]
    B_T, B_O = 4, 6
    with ExitStack() as ctx:
        al = Buffers(nc, ctx, "mlp")
        w1 = al.sb("w1", [P, 2, KC, NJ * P], F32R)
        w2 = al.sb("w2", [P, 2, NJ, D], F32R)
        xin = al.sb("xin", [P, TT, D])
        norm = al.sb("norm", [P, TT, D])
        xT = al.sb("xT", [P, 2, KC, S], F32R)
        gf = al.sb("gf", [P, RING, 2 * S])
        with nc.sbuf_tensor("mlp_stage", [P, 4, KC, D], F32) as stage_buf:
            stage = [stage_buf[:, i] for i in range(4)]
        gT = al.sb("gT", [P, 2, NJ, S], F32R)
        xres = al.sb("xres", [P, TT, D])
        xo = al.sb("xo", [P, TT, D])
        rows = {n: al.sb(f"row_{n}", [P, D]) for n in ("g", "b", "ob")}
        stats, mv = al.sb("stats", [P, TT, 6]), al.sb("mv", [P, TT, 2])
        veps, rstd, eps = (al.sb(n, [P, TT]) for n in ("veps", "rstd", "eps"))
        dummy = al.sb("dummy", [P, 1])
        sem = {n: al.sem(n) for n in ("w_in0 w_in1 w_in2 w_in3 row_in x_in xres_in out_st w_hi w_lo pe_x act_x dve_x pe_fc act_g act_gh dve_g "
                                      "pe_o dve_o eps_set dve_bs dve_mv pool_ve pool_rs dve_xn pool_g pool_b pool_res").split()}
        block = ctx.enter_context(nc.Block())
        W1, W2 = A["L0_xattn_fc_w"], A["L0_xattn_proj_w"]
        wunits = [(W1[:, i * D:(i + 1) * D].rearrange("(k p) n -> p k n", p=P),
                   [w1[:, hl, :, i * D:(i + 1) * D] for hl in range(2)]) for i in range(4)]
        wunits += [(W2[i * D:(i + 1) * D, :].rearrange("(k p) n -> p k n", p=P),
                    [w2[:, hl, 4 * i:4 * i + 4, :] for hl in range(2)]) for i in range(4)]
        stage_at = [0, 2, 1, 3, 1, 3, 1, 3]
        fcb = c["col"]["L0_xattn_fc_b"]

        def bodies(eng, body):
            body(0, True)
            with eng.Fori(1, NB - 1) as v:
                body(v, True)
            body(NB - 1, False)

        @block.sync
        def _(sp):
            sp.dma_start(xin[:], rows_of(x_in, 0)).then_inc(sem["x_in"], 16)
            for n, src in (("g", "L0_xattn_ln2_w"), ("b", "L0_xattn_ln2_b"), ("ob", "L0_xattn_proj_b")):
                sp.dma_start(rows[n][:], A[src].partition_broadcast(P)).then_inc(sem["row_in"], 16)
            for j, (src, _) in enumerate(wunits):
                if j >= 4:
                    sp.wait_ge(sem["w_lo"], j - 1)
                sp.dma_start(stage[stage_at[j]], src).then_inc(sem[f"w_in{stage_at[j]}"], 16)

            def body(v, N):
                if N:
                    sp.wait_ge(sem["dve_xn"], v * TT + TT)
                    sp.dma_start(xin[:], rows_of(x_in, v + 1)).then_inc(sem["x_in"], 16)
                wait(sp, sem["dve_o"], v * TT)
                sp.dma_start(xres[:], rows_of(x_in, v)).then_inc(sem["xres_in"], 16)
                sp.wait_ge(sem["dve_o"], v * TT + TT)
                sp.dma_start(rows_of(x_out, v), xo[:]).then_inc(sem["out_st"], 16)

            bodies(sp, body)
            sp.wait_ge(sem["out_st"], 16 * NB)

        @block.gpsimd
        def _(pool):
            nc.gpsimd.memset(eps[:], 1e-5).then_inc(sem["eps_set"], 1)
            pool.wait_ge(sem["eps_set"], 1)

            def norm_rows(n):
                pool.wait_ge(sem["dve_mv"], n * TT + TT)
                nc.gpsimd.tensor_tensor(veps[:], mv[:, :, 1], eps[:], ALU.add).then_inc(sem["pool_ve"], 1)
                pool.wait_ge(sem["pool_ve"], n + 1)
                nc.gpsimd.tensor_tensor(rstd[:], veps[:], c["half"][:, 0:TT], ALU.pow).then_inc(sem["pool_rs"], 1)
                if isinstance(n, int) and n == 0:
                    pool.wait_ge(sem["row_in"], 48)
                for t in range(TT):
                    pool.wait_ge(sem["dve_xn"], n * TT + (t + 1))
                    nc.gpsimd.tensor_tensor(norm[:, t], norm[:, t], rows["g"][:], ALU.mult).then_inc(sem["pool_g"], 1)
                    pool.wait_ge(sem["pool_g"], n * TT + (t + 1))
                    nc.gpsimd.tensor_tensor(norm[:, t], norm[:, t], rows["b"][:], ALU.add).then_inc(sem["pool_b"], 1)

            norm_rows(0)

            def body(v, N):
                pool.wait_ge(sem["xres_in"], v * 16 + 16)
                for t in range(TT):
                    nc.gpsimd.tensor_tensor(xres[:, t], xres[:, t], rows["ob"][:], ALU.add).then_inc(sem["pool_res"], 1)
                if N:
                    norm_rows(v + 1)

            bodies(pool, body)

        @block.scalar
        def _(act):
            def high_weights(j):
                act.wait_ge(sem[f"w_in{stage_at[j]}"], 16 * (stage_at[:j + 1].count(stage_at[j])))
                nc.scalar.activation(wunits[j][1][HI], stage[stage_at[j]], ACT.Copy).then_inc(sem["w_hi"], 1)

            high_weights(0)

            def high(n, t):
                act.wait_ge(sem["pe_x"], n * TT + (t + 1))
                nc.scalar.activation(xT[:, HI, :, t * P:(t + 1) * P], ps[:, B_T + t, :].rearrange("p (k s) -> p k s", k=KC),
                                     ACT.Copy).then_inc(sem["act_x"], 1)

            high_weights(1)
            for t in range(TT):
                high(0, t)
            high_weights(2)
            high_weights(3)

            def body(v, N):
                for q in range(NQ):
                    if isinstance(v, int) and v == 0:
                        if q < 4:
                            high_weights(4 + q)
                        if q == 4:
                            act.wait_ge(sem["w_lo"], len(wunits))
                    act.wait_ge(sem["pe_fc"], v * NQ + (q + 1))
                    if q >= RING:
                        act.wait_ge(sem["dve_g"], v * NQ + (q - RING + 1))
                    for i in range(2):
                        last = nc.scalar.activation(gf[:, q % RING, i * S:(i + 1) * S], ps[:, q % RING, i * S:(i + 1) * S],
                                                    ACT.Gelu_apprx_tanh, bias=c["cols"][:, fcb + 2 * q + i:fcb + 2 * q + i + 1])
                    last.then_inc(sem["act_g"], 1)
                    act.wait_ge(sem["act_g"], v * NQ + (q + 1))
                    nc.scalar.activation(gT[:, HI, 2 * q:2 * q + 2, :], gf[:, q % RING].rearrange("p (j s) -> p j s", j=2),
                                         ACT.Copy).then_inc(sem["act_gh"], 1)
                if N:
                    for t in range(TT):
                        high(v + 1, t)

            bodies(act, body)

        @block.vector
        def _(dve):
            def norm_stats(n):
                dve.wait_ge(sem["x_in"], n * 16 + 16)
                for t in range(TT):
                    nc.vector.bn_stats(stats[:, t], xin[:, t]).then_inc(sem["dve_bs"], 1)
                dve.wait_ge(sem["dve_bs"], n * TT + TT)
                nc.vector.memset(dummy[:], 0.0)
                for t in range(TT):
                    nc.vector.bn_aggr(mv[:, t], stats[:, t]).then_inc(sem["dve_mv"], 1)

            def norm_apply(n):
                dve.wait_ge(sem["pool_rs"], n + 1)
                wait(dve, sem["pe_x"], n * TT)
                for t in range(TT):
                    nc.vector.tensor_scalar(norm[:, t], xin[:, t], mv[:, t, 0:1], rstd[:, t:t + 1],
                                            ALU.subtract, ALU.mult).then_inc(sem["dve_xn"], 1)

            norm_stats(0)
            norm_apply(0)

            def low_weights(j):
                dve.wait_ge(sem["w_hi"], j + 1)
                dst = wunits[j][1]
                nc.vector.tensor_tensor(dst[LO], stage[stage_at[j]], dst[HI], ALU.subtract).then_inc(sem["w_lo"], 1)

            low_weights(0)

            def low(n, t):
                dve.wait_ge(sem["act_x"], n * TT + (t + 1))
                nc.vector.tensor_tensor(xT[:, LO, :, t * P:(t + 1) * P], ps[:, B_T + t, :].rearrange("p (k s) -> p k s", k=KC),
                                        xT[:, HI, :, t * P:(t + 1) * P], ALU.subtract).then_inc(sem["dve_x"], 1)

            low_weights(1)
            for t in range(TT):
                low(0, t)
            low_weights(2)
            low_weights(3)

            def body(v, N):
                for q in range(NQ):
                    if isinstance(v, int) and v == 0 and q < 4:
                        low_weights(4 + q)
                    if N and q == 1:
                        norm_stats(v + 1)
                    if N and q == 2:
                        norm_apply(v + 1)
                    dve.wait_ge(sem["act_gh"], v * NQ + (q + 1))
                    nc.vector.tensor_tensor(gT[:, LO, 2 * q:2 * q + 2, :], gf[:, q % RING].rearrange("p (j s) -> p j s", j=2),
                                            gT[:, HI, 2 * q:2 * q + 2, :], ALU.subtract).then_inc(sem["dve_g"], 1)
                if N:
                    for t in range(TT):
                        low(v + 1, t)
                wait(dve, sem["out_st"], v * 16)
                dve.wait_ge(sem["pool_res"], v * TT + TT)
                for t in range(TT):
                    dve.wait_ge(sem["pe_o"], v * TT + (t + 1))
                    nc.vector.tensor_tensor(xo[:, t], ps[:, B_O + t, :], xres[:, t], ALU.add).then_inc(sem["dve_o"], 1)

            bodies(dve, body)

        @block.tensor
        def _(pe):
            def turn(n, t):
                for k in range(KC):
                    last = nc.tensor.transpose(ps[:, B_T + t, k * P:(k + 1) * P], norm[:, t, k * P:(k + 1) * P], ident[:])
                last.then_inc(sem["pe_x"], 1)

            for t in range(TT):
                pe.wait_ge(sem["pool_b"], t + 1)
                turn(0, t)

            def body(v, N):
                pe.wait_ge(sem["dve_x"], v * TT + TT)
                for q in range(NQ):
                    if q >= RING:
                        pe.wait_ge(sem["act_g"], v * NQ + (q - RING + 1))
                    if isinstance(v, int) and v == 0 and q % 2 == 0:
                        pe.wait_ge(sem["w_lo"], q // 2 + 1)
                    for i in range(2):
                        j = 2 * q + i
                        for a, (wa, xa) in enumerate(PAIRS):
                            for k in range(KC):
                                last = nc.tensor.matmul(ps[:, q % RING, i * S:(i + 1) * S], w1[:, wa, k, j * P:(j + 1) * P], xT[:, xa, k, :],
                                                        start=(a == 0 and k == 0), stop=(a == 2 and k == KC - 1))
                    last.then_inc(sem["pe_fc"], 1)
                wait(pe, sem["dve_o"], v * TT)
                for t in range(TT):
                    if N and t == 1:
                        pe.wait_ge(sem["pool_b"], v * TT + 2 * TT)
                        for tt in range(TT):
                            turn(v + 1, tt)
                    for j in range(NJ):
                        if isinstance(v, int) and v == 0 and t == 0 and j % 4 == 0:
                            pe.wait_ge(sem["w_lo"], 4 + j // 4 + 1)
                        if t == 0 and j % 2 == 0:
                            pe.wait_ge(sem["dve_g"], v * NQ + (j // 2 + 1))
                        for a, (ga, wa) in enumerate(PAIRS):
                            last = nc.tensor.matmul(ps[:, B_O + t, :], gT[:, ga, j, t * P:(t + 1) * P], w2[:, wa, j, :],
                                                    start=(a == 0 and j == 0), stop=(a == 2 and j == NJ - 1))
                    last.then_inc(sem["pe_o"], 1)

            bodies(pe, body)


def single_head_phase(nc, c, A, x_in, x_out):
    ps, ident = c["ps"], c["ident"]
    B_G, B_V, B_S, B_PT = 0, 2, 4, 5
    B_O = (6, 5)
    B_T = ((7, 6), (7, 5))
    with ExitStack() as ctx:
        al = Buffers(nc, ctx, "l1")
        raw = {n: al.sb(f"raw_{n}", [P, KC, D]) for n in "qkvo"}
        woT = al.sb("woT", [P, KC, D])
        a1 = al.sb("a1", [P, 2, KC, D], F32R)
        a2 = al.sb("a2", [P, 2, KC, D], F32R)
        xin, cin = al.sb("xin", [P, TT, D]), al.sb("cin", [P, TT, D])
        xT, cT = al.sb("xT", [P, 2, KC, S], F32R), al.sb("cT", [P, 2, KC, S], F32R)
        G = al.sb("G", [P, 2, KC, S], F32R)
        VO = al.sb("VO", [P, 2, TT, D], F32R)
        Pb = al.sb("Pb", [P, TT, S])
        PT = al.sb("PT", [P, 2, TT, S], F32R)
        xres, xo = al.sb("xres", [P, TT, D]), al.sb("xo", [P, TT, D])
        alpha = al.sb("alpha", [P, 1])
        negmax, sums, rcp, fac = (al.sb(n, [P, TT]) for n in ("negmax", "sums", "rcp", "fac"))
        sem = {n: al.sem(n) for n in ("w_in_q w_in_k w_in_v w_in_o al_in x_in c_in xres_in out_st pe_wt act_wt pe_a act_a dve_a pe_T act_T dve_T pe_G act_G "
                                      "dve_G pe_V act_V dve_V pe_S dve_max act_exp pe_PT act_PT dve_PT pe_O dve_O dve_rc dve_fac").split()}
        block = ctx.enter_context(nc.Block())
        names = {"q": "L1_xattn_w_q", "k": "L1_xattn_w_k", "v": "L1_xattn_w_v", "o": "L1_xattn_w_o"}

        def bodies(eng, body):
            body(0, None, True, False, True)
            with eng.Fori(0, NB - 2) as u:
                body(u + 1, u, True, True, True)
            body(NB - 1, NB - 2, True, True, False)
            body(NB, NB - 1, False, True, False)

        @block.sync
        def _(sp):
            sp.dma_start(cin[:], rows_of(A["ctx_2048"], 0)).then_inc(sem["c_in"], 16)
            for n in "kqov":
                sp.dma_start(raw[n][:], A[names[n]].rearrange("(k p) n -> p k n", p=P)).then_inc(sem[f"w_in_{n}"], 16)
            sp.dma_start(alpha[:], A["L1_xattn_alpha"].partition_broadcast(P)).then_inc(sem["al_in"], 16)
            sp.dma_start(xin[:], rows_of(x_in, 0)).then_inc(sem["x_in"], 16)

            def body(vf, vb, F, B, N):
                if N:
                    sp.wait_ge(sem["pe_T"], vf * (2 * TT) + 2 * TT)
                    sp.dma_start(xin[:], rows_of(x_in, vf + 1)).then_inc(sem["x_in"], 16)
                    sp.dma_start(cin[:], rows_of(A["ctx_2048"], vf + 1)).then_inc(sem["c_in"], 16)
                if B:
                    wait(sp, sem["dve_O"], vb * TT)
                    sp.dma_start(xres[:], rows_of(x_in, vb)).then_inc(sem["xres_in"], 16)
                    sp.wait_ge(sem["dve_O"], vb * TT + TT)
                    sp.dma_start(rows_of(x_out, vb), xo[:]).then_inc(sem["out_st"], 16)

            bodies(sp, body)
            sp.wait_ge(sem["out_st"], 16 * NB)

        @block.scalar
        def _(act):
            def high(n, which, dst, t):
                act.wait_ge(sem["pe_T"], n * (2 * TT) + (which * TT + t + 1))
                nc.scalar.activation(dst[:, HI, :, t * P:(t + 1) * P], ps[:, B_T[which][t], :].rearrange("p (k s) -> p k s", k=KC),
                                     ACT.Copy).then_inc(sem["act_T"], 1)

            def high_folded(i, dst, scale):
                for k in range(KC):
                    act.wait_ge(sem["pe_a"], i * KC + k + 1)
                    nc.scalar.activation(dst[:, HI, k], ps[:, k, :], ACT.Copy, scale=scale).then_inc(sem["act_a"], 1)

            for t in range(TT):
                high(0, 0, cT, t)
            high_folded(0, a1, D ** -0.5)
            for k in range(KC):
                act.wait_ge(sem["pe_wt"], k + 1)
                nc.scalar.activation(woT[:, k], ps[:, 4 + k, :], ACT.Copy).then_inc(sem["act_wt"], 1)
            high_folded(1, a2, 1.0)
            for t in range(TT):
                high(0, 1, xT, t)

            def body(vf, vb, F, B, N):
                for i in range(2):
                    if F:
                        act.wait_ge(sem["pe_G"], vf * 2 + (i + 1))
                        nc.scalar.activation(G[:, HI, 2 * i:2 * i + 2], ps[:, B_G + i, :].rearrange("p (k s) -> p k s", k=2),
                                             ACT.Copy).then_inc(sem["act_G"], 1)
                    if B and i == 0:
                        act.wait_ge(sem["pe_PT"], vb + 1)
                        nc.scalar.activation(PT[:, HI], ps[:, B_PT, :].rearrange("p (k s) -> p k s", k=TT),
                                             ACT.Copy).then_inc(sem["act_PT"], 1)
                if F:
                    for t in range(TT):
                        act.wait_ge(sem["pe_V"], vf * TT + (t + 1))
                        nc.scalar.activation(VO[:, HI, t], ps[:, B_V + t, :], ACT.Copy).then_inc(sem["act_V"], 1)
                if N:
                    for t in range(TT):
                        high(vf + 1, 0, cT, t)
                if F:
                    act.wait_ge(sem["dve_max"], vf + 1)
                    for t in range(TT):
                        last = nc.scalar.activation(Pb[:, t], ps[:, B_S, t * S:(t + 1) * S], ACT.Exp, bias=negmax[:, t:t + 1],
                                                    accum_out=sums[:, t:t + 1])
                    last.then_inc(sem["act_exp"], 1)
                if N:
                    for t in range(TT):
                        high(vf + 1, 1, xT, t)

            bodies(act, body)

        @block.vector
        def _(dve):
            def low(n, which, dst, t):
                dve.wait_ge(sem["act_T"], n * (2 * TT) + (which * TT + t + 1))
                nc.vector.tensor_tensor(dst[:, LO, :, t * P:(t + 1) * P], ps[:, B_T[which][t], :].rearrange("p (k s) -> p k s", k=KC),
                                        dst[:, HI, :, t * P:(t + 1) * P], ALU.subtract).then_inc(sem["dve_T"], 1)

            def low_folded(i, dst, scale):
                for k in range(KC):
                    dve.wait_ge(sem["act_a"], i * KC + k + 1)
                    nc.vector.scalar_tensor_tensor(dst[:, LO, k], ps[:, k, :], scale, dst[:, HI, k],
                                                   ALU.mult, ALU.subtract).then_inc(sem["dve_a"], 1)

            for t in range(TT):
                low(0, 0, cT, t)
            low_folded(0, a1, D ** -0.5)
            low_folded(1, a2, 1.0)
            for t in range(TT):
                low(0, 1, xT, t)
            dve.wait_ge(sem["al_in"], 16)

            def body(vf, vb, F, B, N):
                for i in range(2):
                    if F:
                        dve.wait_ge(sem["act_G"], vf * 2 + (i + 1))
                        nc.vector.tensor_tensor(G[:, LO, 2 * i:2 * i + 2], ps[:, B_G + i, :].rearrange("p (k s) -> p k s", k=2),
                                                G[:, HI, 2 * i:2 * i + 2], ALU.subtract).then_inc(sem["dve_G"], 1)
                    if B and i == 0:
                        dve.wait_ge(sem["act_PT"], vb + 1)
                        nc.vector.tensor_tensor(PT[:, LO], ps[:, B_PT, :].rearrange("p (k s) -> p k s", k=TT),
                                                PT[:, HI], ALU.subtract).then_inc(sem["dve_PT"], 1)
                        nc.vector.reciprocal(rcp[:], sums[:]).then_inc(sem["dve_rc"], 1)
                if B:
                    dve.wait_ge(sem["dve_rc"], vb + 1)
                    nc.vector.tensor_scalar(fac[:], rcp[:], alpha[:, 0:1], None, ALU.mult).then_inc(sem["dve_fac"], 1)
                    dve.wait_ge(sem["dve_fac"], vb + 1)
                    dve.wait_ge(sem["xres_in"], vb * 16 + 16)
                    wait(dve, sem["out_st"], vb * 16)
                    for t in range(TT):
                        dve.wait_ge(sem["pe_O"], vb * TT + (t + 1))
                        nc.vector.scalar_tensor_tensor(xo[:, t], ps[:, B_O[t], :], fac[:, t:t + 1], xres[:, t],
                                                       ALU.mult, ALU.add).then_inc(sem["dve_O"], 1)
                if F:
                    for t in range(TT):
                        dve.wait_ge(sem["act_V"], vf * TT + (t + 1))
                        nc.vector.tensor_tensor(VO[:, LO, t], ps[:, B_V + t, :], VO[:, HI, t], ALU.subtract).then_inc(sem["dve_V"], 1)
                if N:
                    for t in range(TT):
                        low(vf + 1, 0, cT, t)
                if F:
                    dve.wait_ge(sem["pe_S"], vf + 1)
                    nc.vector.tensor_reduce(negmax[:], ps[:, B_S, :].rearrange("p (t s) -> p t s", t=TT), AX_X, ALU.max,
                                            negate=True).then_inc(sem["dve_max"], 1)
                if N:
                    for t in range(TT):
                        low(vf + 1, 1, xT, t)

            bodies(dve, body)

        @block.tensor
        def _(pe):
            def turn(n, which, src, t, behind):
                if which == 0 and t == 0:
                    wait(pe, sem["dve_T"], n * (2 * TT) - 1 if behind is None else behind * (2 * TT) + (2 * TT + 3))
                elif t == 0:
                    pe.wait_ge(sem["dve_T"], n * (2 * TT) + 1)
                elif behind is not None:
                    pe.wait_ge(sem["dve_O"], behind * TT + (which + 1))
                for k in range(KC):
                    last = nc.tensor.transpose(ps[:, B_T[which][t], k * P:(k + 1) * P], src[:, t, k * P:(k + 1) * P], ident[:])
                last.then_inc(sem["pe_T"], 1)

            def turn_all(n, which, behind=None):
                pe.wait_ge(sem["x_in" if which else "c_in"], n * 16 + 16)
                for t in range(TT):
                    turn(n, which, xin if which else cin, t, behind)

            def fold(l, r):
                for j in range(KC):
                    for o in range(KC):
                        last = nc.tensor.matmul(ps[:, j, :], l[:, o, j * P:(j + 1) * P], r[:, o, :], start=(o == 0), stop=(o == KC - 1))
                    last.then_inc(sem["pe_a"], 1)

            turn_all(0, 0)
            pe.wait_ge(sem["w_in_k"], 16)
            pe.wait_ge(sem["w_in_q"], 16)
            fold(raw["k"], raw["q"])
            pe.wait_ge(sem["w_in_o"], 16)
            pe.wait_ge(sem["dve_T"], TT)
            for k in range(KC):
                for o in range(KC):
                    last = nc.tensor.transpose(ps[:, 4 + k, o * P:(o + 1) * P], raw["o"][:, o, k * P:(k + 1) * P], ident[:])
                last.then_inc(sem["pe_wt"], 1)
            pe.wait_ge(sem["w_in_v"], 16)
            pe.wait_ge(sem["act_wt"], KC)
            pe.wait_ge(sem["dve_a"], KC)
            fold(raw["v"], woT)
            turn_all(0, 1)
            pe.wait_ge(sem["dve_a"], 2 * KC)

            def body(vf, vb, F, B, N):
                if F:
                    pe.wait_ge(sem["dve_T"], vf * (2 * TT) + TT)
                for i in range(2):
                    if F:
                        if B:
                            pe.wait_ge(sem["dve_G"], vb * 2 + (i + 1))
                        for k2 in range(2):
                            m = 2 * i + k2
                            for a, (wa, ca) in enumerate(PAIRS):
                                for k in range(KC):
                                    last = nc.tensor.matmul(ps[:, B_G + i, k2 * S:(k2 + 1) * S], a1[:, wa, k, m * P:(m + 1) * P],
                                                            cT[:, ca, k, :], start=(a == 0 and k == 0), stop=(a == 2 and k == KC - 1))
                        last.then_inc(sem["pe_G"], 1)
                    if B and i == 0:
                        pe.wait_ge(sem["act_exp"], vb + 1)
                        pe.wait_ge(sem["dve_T"], (vb * (2 * TT) + 4 * TT) if F else NB * (2 * TT))
                        for kt in range(TT):
                            for t in range(TT):
                                last = nc.tensor.transpose(ps[:, B_PT, kt * S + t * P:kt * S + (t + 1) * P],
                                                           Pb[:, t, kt * P:(kt + 1) * P], ident[:])
                        last.then_inc(sem["pe_PT"], 1)
                if B:
                    pe.wait_ge(sem["dve_PT"], vb + 1)
                    pe.wait_ge(sem["dve_V"], vb * TT + TT)
                    for t in range(TT):
                        for a, (pa, va) in enumerate(PAIRS):
                            for kt in range(TT):
                                last = nc.tensor.matmul(ps[:, B_O[t], :], PT[:, pa, kt, t * P:(t + 1) * P], VO[:, va, kt, :],
                                                        start=(a == 0 and kt == 0), stop=(a == 2 and kt == TT - 1))
                        last.then_inc(sem["pe_O"], 1)
                if F:
                    for t in range(TT):
                        if B:
                            pe.wait_ge(sem["dve_V"], vb * TT + (t + 1))
                        for a, (ca, wa) in enumerate(PAIRS):
                            for k in range(KC):
                                last = nc.tensor.matmul(ps[:, B_V + t, :], cT[:, ca, k, t * P:(t + 1) * P], a2[:, wa, k, :],
                                                        start=(a == 0 and k == 0), stop=(a == 2 and k == KC - 1))
                        last.then_inc(sem["pe_V"], 1)
                if N:
                    turn_all(vf + 1, 0, vb)
                if F:
                    pe.wait_ge(sem["dve_G"], vf * 2 + 2)
                    pe.wait_ge(sem["dve_T"], vf * (2 * TT) + 2 * TT)
                    wait(pe, sem["act_exp"], vf)
                    for t in range(TT):
                        for a, (xa, ga) in enumerate(PAIRS):
                            for k in range(KC):
                                last = nc.tensor.matmul(ps[:, B_S, t * S:(t + 1) * S], xT[:, xa, k, t * P:(t + 1) * P], G[:, ga, k, :],
                                                        start=(a == 0 and k == 0), stop=(a == 2 and k == KC - 1))
                    last.then_inc(sem["pe_S"], 1)
                if N:
                    turn_all(vf + 1, 1, vb)

            bodies(pe, body)


def build(nc, A, out, only=None):
    with ExitStack() as ctx:
        def scratch(name, shape):
            return nc.dram_tensor(name, shape, F32, kind="Internal").ap()

        c = {"col": {}}
        c["ident"] = ctx.enter_context(nc.sbuf_tensor("ident", [P, P], F32))
        c["cols"] = ctx.enter_context(nc.sbuf_tensor("cols", [P, 32], F32))
        c["half"] = ctx.enter_context(nc.sbuf_tensor("half", [P, 8], F32))
        c["ps"] = ctx.enter_context(nc.psum_tensor("ps", [P, 8, BANK], F32))
        c["mask_stored"] = nc.alloc_semaphore(name="mask_stored")
        m_rows = [ctx.enter_context(nc.sbuf_tensor(f"mask_row{i}", [NB, S], F32)) for i in range(2)]
        c["mask_rows"] = m_rows
        c["mask_min"] = scratch("mask_min", (NB, 4 * S))
        c["mask_inf"] = scratch("mask_inf", (NB, 4 * S))
        c["scr"] = [scratch(f"split{g}", (P, 4, S)) for g in range(STEPS)]
        c["scrk"] = scratch("split_k", (P, 2, S))
        hid = [scratch(f"hidden{i}", (NB * S, D)) for i in range(4)]

        setup_phase(nc, c, A)

        mha = {"heads": 16, "hd": 32, "gqa": False, "nk": D, "ot": S, "post_ln": False, "eps": 1e-5, "qscale": 32.0 ** -0.5}
        l0 = ({
            **mha, "tag": "l0", "x_in": A["x"], "x_out": hid[0], "transposed": False, "ln_x": True, "ln_c": False, "oscale": 1.0,
            "wq": "L0_xattn_q_w", "wk": "L0_xattn_k_w", "wv": "L0_xattn_v_w", "wo": "L0_xattn_cproj_w", "mask": c["mask_min"],
            "qcol": c["col"]["L0_xattn_q_b"], "kcol": c["col"]["L0_xattn_k_b"],
            "rows": [("g", "L0_xattn_ln1_w", D), ("b", "L0_xattn_ln1_b", D), ("vb", "L0_xattn_v_b", D), ("ob", "L0_xattn_cproj_b", D)]})
        l2 = ({
            "tag": "l2", "heads": 32, "hd": 16, "gqa": True, "nk": P, "ot": BANK, "post_ln": True, "eps": 1e-6, "qscale": 0.25,
            "x_in": hid[2], "x_out": hid[3], "transposed": False, "ln_x": False, "ln_c": False, "oscale": 1.0,
            "wq": "L2_xattn_Wq", "wk": "L2_xattn_Wk", "wv": "L2_xattn_Wv", "wo": "L2_xattn_Wo",
            "qcol": c["col"]["L2_xattn_bq"], "kcol": c["col"]["L2_xattn_bk"],
            "rows": [("g", "L2_xattn_gamma", D), ("b", "L2_xattn_beta", D), ("vb", "L2_xattn_bv", P), ("ob", "L2_xattn_bo", D)]})
        l3 = ({
            **mha, "tag": "l3", "x_in": hid[3], "x_out": out, "transposed": True, "ln_x": False, "ln_c": True, "oscale": None,
            "wq": "L3_xattn_Wq", "wk": "L3_xattn_Wk", "wv": "L3_xattn_Wv", "wo": "L3_xattn_Wo", "mask": c["mask_inf"],
            "qcol": None, "kcol": None,
            "rows": [("g", "L3_xattn_ln_gamma", D), ("b", "L3_xattn_ln_beta", D)]})
        if only in ("l0", "l2", "l3"):
            L = {"l0": l0, "l2": l2, "l3": l3}[only]
            attention_phase(nc, c, A, {**L, "x_in": A["hin"], "x_out": out})
        elif only == "mlp":
            mlp_phase(nc, c, A, A["hin"], out)
        elif only == "l1":
            single_head_phase(nc, c, A, A["hin"], out)
        else:
            attention_phase(nc, c, A, l0)
            mlp_phase(nc, c, A, hid[0], hid[1])
            single_head_phase(nc, c, A, hid[1], hid[2])
            attention_phase(nc, c, A, l2)
            attention_phase(nc, c, A, l3)


def kernel(**inputs):
    import numpy as _np
    import concourse.bacc as _bacc
    from concourse import mybir as _mybir
    from concourse.bass_utils import run_bass_kernel_spmd as _run

    flat = {"x": (NB * S, D), "ctx_2048": (NB * S, D), "mask_Bx1xSxS2_ff0": (NB * S, S), "L1_xattn_alpha": (1,)}
    nc = _bacc.Bacc("TRN2", target_bir_lowering=False, num_devices=1)
    arrays, aps = {}, {}
    for name, a in inputs.items():
        a = _np.ascontiguousarray(a)
        if name in flat:
            a = a.reshape(flat[name])
        if name == "mask_BxS2_bf1":
            a = a.view(_np.uint8)
        arrays[f"in_{name}"] = a
        aps[name] = nc.dram_tensor(f"in_{name}", a.shape, _mybir.dt.from_np(a.dtype), kind="ExternalInput").ap()
    out = nc.dram_tensor("out_x", (NB * S, D), F32, kind="ExternalOutput").ap()
    build(nc, aps, out)
    r = _run(nc, [arrays], core_ids=[0])
    return r.results[0]["out_x"].reshape(NB, S, D)
```
